# Optimizing a Trainium2 kernel written in Bass

```python
import numpy as np
import jax
import jax.numpy as jnp

def _softmax(x, axis=-1):
    return jax.nn.softmax(x, axis=axis)

def _gelu(x):
    return jax.nn.gelu(x, approximate=True)

def _silu(x):
    return jax.nn.silu(x)

def _sigmoid(x):
    return jax.nn.sigmoid(x)

def _layernorm(x, axis=-1, eps=1e-05):
    m = jnp.mean(x, axis=axis, keepdims=True)
    v = jnp.var(x, axis=axis, keepdims=True)
    return (x - m) / jnp.sqrt(v + eps)

def _scatter_add(tgt, idx, src, axis=0):
    return tgt.at[idx].add(src)

def _segment_sum(src, seg, n):
    return jax.ops.segment_sum(src, seg, n)
kernel_name = 'mk_seq_preln_d1_jaxref_r8_177d91'

def setup_inputs(seed: int=0):
    np.random.seed(seed)
    _w = jnp.asarray

    def _L0_attn_setup():
        import jax, jax.numpy as jnp
        import numpy as np
        DT_RANK = 64
        N_STATES = 16

        def selective_scan(u, delta, A, B, C, D):
            dA = jnp.einsum('bld,dn->bldn', delta, A)
            dB_u = jnp.einsum('bld,bld,bln->bldn', delta, u, B)
            dA_shift = jnp.concatenate([dA[:, 1:], jnp.zeros_like(dA[:, :1])], axis=1)
            dA_cumsum = jnp.exp(jnp.flip(jnp.cumsum(jnp.flip(dA_shift, axis=1), axis=1), axis=1))
            xs = jnp.cumsum(dB_u * dA_cumsum, axis=1) / (dA_cumsum + 1e-12)
            y = jnp.einsum('bldn,bln->bld', xs, C)
            return y + u * D
        key = jax.random.key(seed)
        ks = jax.random.split(key, 6)
        b, l, d = (2, 128, 128)
        dt_rank, n = (DT_RANK, N_STATES)
        x = jax.random.normal(ks[0], (b, l, d), dtype=jnp.float32)
        W_x = jax.random.normal(ks[1], (d, dt_rank + 2 * n), dtype=jnp.float32) * (1.0 / np.sqrt(d))
        W_dt = jax.random.normal(ks[2], (dt_rank, d), dtype=jnp.float32) * (1.0 / np.sqrt(dt_rank))
        b_dt = jnp.zeros((d,), dtype=jnp.float32)
        A_log = jnp.log(jnp.tile(jnp.arange(1, n + 1, dtype=jnp.float32)[None, :], (d, 1)))
        D = jnp.ones((d,), dtype=jnp.float32)
        W_out = jax.random.normal(ks[3], (d, d), dtype=jnp.float32) * (1.0 / np.sqrt(d))
        b_out = jnp.zeros((d,), dtype=jnp.float32)
        return {'x': x, 'W_x': W_x, 'W_dt': W_dt, 'b_dt': b_dt, 'A_log': A_log, 'D': D, 'W_out': W_out, 'b_out': b_out}
    _L0_attn_in = _L0_attn_setup()

    def _L0_ffn_setup():
        import jax, jax.numpy as jnp
        import numpy as np
        E = 8
        K = 2
        key = jax.random.key(seed)
        ks = jax.random.split(key, 8)
        B, T, d = (4, 256, 128)
        h = 4 * d // E
        s = 0.02
        X = jax.random.normal(ks[0], (B, T, d), jnp.float32)
        routing_W = jax.random.normal(ks[1], (E, d), jnp.float32) * s
        expert_bias = jnp.zeros((E,), jnp.float32)
        sW1 = jax.random.normal(ks[2], (d, h), jnp.float32) * s
        sb1 = jnp.zeros((h,), jnp.float32)
        sW2 = jax.random.normal(ks[3], (h, d), jnp.float32) * s
        sb2 = jnp.zeros((d,), jnp.float32)
        rW1 = jax.random.normal(ks[4], (E, d, h), jnp.float32) * s
        rb1 = jnp.zeros((E, h), jnp.float32)
        rW2 = jax.random.normal(ks[5], (E, h, d), jnp.float32) * s
        rb2 = jnp.zeros((E, d), jnp.float32)
        return dict(X=X, routing_W=routing_W, expert_bias=expert_bias, sW1=sW1, sb1=sb1, sW2=sW2, sb2=sb2, rW1=rW1, rb1=rb1, rW2=rW2, rb2=rb2)
    _L0_ffn_in = _L0_ffn_setup()
    _d = {'L0_attn_x': _L0_attn_in['x'], 'L0_attn_W_x': _L0_attn_in['W_x'], 'L0_attn_W_dt': _L0_attn_in['W_dt'], 'L0_attn_b_dt': _L0_attn_in['b_dt'], 'L0_attn_A_log': _L0_attn_in['A_log'], 'L0_attn_D': _L0_attn_in['D'], 'L0_attn_W_out': _L0_attn_in['W_out'], 'L0_attn_b_out': _L0_attn_in['b_out'], 'L0_ffn_routing_W': _L0_ffn_in['routing_W'], 'L0_ffn_expert_bias': _L0_ffn_in['expert_bias'], 'L0_ffn_sW1': _L0_ffn_in['sW1'], 'L0_ffn_sb1': _L0_ffn_in['sb1'], 'L0_ffn_sW2': _L0_ffn_in['sW2'], 'L0_ffn_sb2': _L0_ffn_in['sb2'], 'L0_ffn_rW1': _L0_ffn_in['rW1'], 'L0_ffn_rb1': _L0_ffn_in['rb1'], 'L0_ffn_rW2': _L0_ffn_in['rW2'], 'L0_ffn_rb2': _L0_ffn_in['rb2']}
    _x0 = _d['L0_attn_x']
    _d['L0_attn_x'] = jax.random.normal(jax.random.fold_in(jax.random.key(seed), 1), (4, 1024, 128), dtype=_x0.dtype)
    del _x0
    return _d

def reference(L0_attn_x, L0_attn_W_x, L0_attn_W_dt, L0_attn_b_dt, L0_attn_A_log, L0_attn_D, L0_attn_W_out, L0_attn_b_out, L0_ffn_routing_W, L0_ffn_expert_bias, L0_ffn_sW1, L0_ffn_sb1, L0_ffn_sW2, L0_ffn_sb2, L0_ffn_rW1, L0_ffn_rb1, L0_ffn_rW2, L0_ffn_rb2):

    def _L0_attn_ref(x, W_x, W_dt, b_dt, A_log, D, W_out, b_out):
        import jax, jax.numpy as jnp
        import numpy as np
        DT_RANK = 64
        N_STATES = 16

        def selective_scan(u, delta, A, B, C, D):
            dA = jnp.einsum('bld,dn->bldn', delta, A)
            dB_u = jnp.einsum('bld,bld,bln->bldn', delta, u, B)
            dA_shift = jnp.concatenate([dA[:, 1:], jnp.zeros_like(dA[:, :1])], axis=1)
            dA_cumsum = jnp.exp(jnp.flip(jnp.cumsum(jnp.flip(dA_shift, axis=1), axis=1), axis=1))
            xs = jnp.cumsum(dB_u * dA_cumsum, axis=1) / (dA_cumsum + 1e-12)
            y = jnp.einsum('bldn,bln->bld', xs, C)
            return y + u * D
        n = A_log.shape[1]
        A = -jnp.exp(A_log)
        x_dbl = jnp.einsum('bld,de->ble', x, W_x)
        delta = x_dbl[..., :DT_RANK]
        B = x_dbl[..., DT_RANK:DT_RANK + n]
        C = x_dbl[..., DT_RANK + n:]
        delta = jax.nn.softplus(jnp.einsum('blr,rd->bld', delta, W_dt) + b_dt)
        y = selective_scan(x, delta, A, B, C, D)
        return jnp.einsum('bld,de->ble', y, W_out) + b_out

    def _L0_ffn_ref(X, routing_W, expert_bias, sW1, sb1, sW2, sb2, rW1, rb1, rW2, rb2):
        import jax, jax.numpy as jnp
        import numpy as np
        E = 8
        K = 2
        B, T, d = X.shape
        shared = jax.nn.silu(X @ sW1 + sb1) @ sW2 + sb2
        logits = jnp.einsum('btd,ed->bte', X, routing_W) + expert_bias
        activation = jnp.sqrt(jax.nn.softplus(logits))
        top_vals, top_idx = jax.lax.top_k(activation, K)
        combine = jnp.sum(jax.nn.one_hot(top_idx, E, dtype=X.dtype) * top_vals[..., None], axis=-2)
        Xf = X.reshape(-1, d)
        cf = combine.reshape(-1, E)
        hdn = jax.nn.silu(jnp.einsum('nd,edh->enh', Xf, rW1) + rb1[:, None, :])
        y = jnp.einsum('enh,ehd->end', hdn, rW2) + rb2[:, None, :]
        routed = jnp.einsum('ne,end->nd', cf, y).reshape(B, T, d)
        return shared + routed
    x = L0_attn_x
    x = x + _L0_attn_ref(_layernorm(x, axis=-1), L0_attn_W_x, L0_attn_W_dt, L0_attn_b_dt, L0_attn_A_log, L0_attn_D, L0_attn_W_out, L0_attn_b_out)
    x = x + _L0_ffn_ref(_layernorm(x, axis=-1), L0_ffn_routing_W, L0_ffn_expert_bias, L0_ffn_sW1, L0_ffn_sb1, L0_ffn_sW2, L0_ffn_sb2, L0_ffn_rW1, L0_ffn_rb1, L0_ffn_rW2, L0_ffn_rb2)
    return x

_drawn_inputs = setup_inputs


def setup_inputs(seed=0):
    import zlib

    import numpy as np

    out = dict(_drawn_inputs(seed))
    spreads = {'L0_attn_b_dt': (0.0, 0.1),
     'L0_attn_D': (1.0, 0.2),
     'L0_attn_b_out': (0.0, 0.1),
     'L0_ffn_expert_bias': (0.0, 0.1),
     'L0_ffn_sb1': (0.0, 0.8),
     'L0_ffn_sb2': (0.0, 0.1),
     'L0_ffn_rb1': (0.0, 0.8),
     'L0_ffn_rb2': (0.0, 0.1)}
    factors = {'L0_ffn_sW1': 4.583, 'L0_ffn_sW2': 4.161, 'L0_ffn_rW1': 3.439, 'L0_ffn_rW2': 3.115}
    for name, (base, spread) in spreads.items():
        noise = np.random.default_rng([zlib.crc32(name.encode()), seed]).standard_normal(out[name].shape)
        drawn = base * np.exp(spread * noise) if base else spread * noise
        out[name] = jnp.asarray(drawn.astype(out[name].dtype))
    for name, factor in factors.items():
        out[name] = (out[name] * factor).astype(out[name].dtype)
    return out
```

```python
from contextlib import ExitStack

import concourse.bass as bass
from concourse import mybir

ALU = mybir.AluOpType
ACT = mybir.ActivationFunctionType
AX = mybir.AxisListType
F32 = mybir.dt.float32
I32 = mybir.dt.int32

P = 128
FREE = 1
LN_EPS = 1e-5
LOG_TINY = 27.631021115928547
UNDERFLOW = -104.0
TIE_DROP = -1e30

CLASSES = [(0, 1, 256, 0, 1), (1, 2, 128, 2, 3), (3, 4, 64, 4, 5), (7, 8, 32, 6, 0), (15, 1, 32, 0, 7)]
C_ORDER = [0, 1, 2, 4, 3]
TAIL = 256


def build(nc, x, W_x, W_dt, b_dt, A_log, D, W_out, b_out, routing_W, expert_bias,
          sW1, sb1, sW2, sb2, rW1, rb1, rW2, rb2, out):
    B, L, DM = x.shape
    R = W_dt.shape[0]
    N = A_log.shape[1]
    E, _, H = rW1.shape
    T = L // P
    TT = TAIL // P
    TH = T // 2
    HT = TH * P
    TB = B * TT
    NB = E * H // P
    EB = P // H
    KX = H + E + 1
    SEG = TAIL + 1
    assert DM == P and H == 64 and N == 16 and L % HT == 0 and B == 4

    offs, total = [], 0
    for _, ns, w, _, _ in CLASSES:
        offs.append(total)
        total += ns * B * w

    ctx = ExitStack()
    with ctx:
        def sb(name, shape, dt=F32):
            return ctx.enter_context(nc.sbuf_tensor(name, shape, dt))

        def sem(name):
            return ctx.enter_context(nc.semaphore(name))

        bank = ctx.enter_context(nc.psum_tensor("bank", [P, 8, 512], F32))

        ident = sb("ident", [P, P])
        ramp = sb("ramp", [P, E])
        mask = sb("mask", [P, B * SEG])
        wx = sb("wx", [P, R + 2 * N])
        wxT = sb("wxT", [R, P])
        wdt = sb("wdt", [R, P])
        wcomb = sb("wcomb", [P, P])
        wout = sb("wout", [P, P])
        dwout = sb("dwout", [P, P])
        alog = sb("alog", [P, N])
        aneg = sb("aneg", [P, N])
        aval = sb("aval", [P, N])
        dcol = sb("dcol", [P, 1])
        bdt = sb("bdt", [P, 1])
        bout = sb("bout", [P, P])
        rw = sb("rw", [E, P])
        rwT = sb("rwT", [P, E])
        ebias = sb("ebias", [P, E])
        w1 = sb("w1", [P, (E + 1) * H])
        b1 = sb("b1", [P, NB + 1])
        w2 = sb("w2", [P, NB + 1, P])
        epsv = sb("epsv", [P, T])
        mhalf = sb("mhalf", [P, T * E])
        phalf = sb("phalf", [P, T * E])
        logt = sb("logt", [P, 1])

        xa = sb("xa", [P, B, T, P])
        ra = sb("ra", [P, B, T, P])

        tst = sb("tst", [P, TB, 6])
        tmv = sb("tmv", [P, TB, 2])
        trs = sb("trs", [P, TB])
        txn = sb("txn", [P, TB, P])
        txT = sb("txT", [P, TB, P])
        tab = sb("tab", [P, B, TAIL])
        tex = sb("tex", [P, B, TAIL])
        tre = sb("tre", [P, B, TAIL])
        tdl = sb("tdl", [P, B, SEG])
        tsu = sb("tsu", [P, B, SEG])
        tw = sb("tw", [P, B, TAIL])
        tbc = sb("tbc", [P, TB, 2 * N])
        gprod = sb("gprod", [P, N, B])
        gmax = sb("gmax", [P, 1])
        gmx1 = sb("gmx1", [1, 1])
        flag = sb("flag", [1, 1], I32)
        fa = sb("fa", [P, total])
        fs = sb("fs", [P, total])
        fv = sb("fv", [P, total])
        red = sb("red", [P, 3, B * P])
        yT = sb("yT", [P, B, TAIL])

        st1 = sb("st1", [P, 2, TH, 6])
        mv1 = sb("mv1", [P, 2, TH, 2])
        rs1 = sb("rs1", [P, 2, TH])
        xn1 = sb("xn1", [P, 2, TH, P])
        xT1 = sb("xT1", [P, 2, TH, P])
        st2 = sb("st2", [P, 2, TH, 6])
        mv2 = sb("mv2", [P, 2, TH, 2])
        rs2 = sb("rs2", [P, 2, TH])
        xn2 = sb("xn2", [P, 2, TH, P])
        xT2 = sb("xT2", [P, 2, HT])
        lg = sb("lg", [P, T, E])
        lga = sb("lga", [P, T, E])
        lge = sb("lge", [P, T, E])
        lgr = sb("lgr", [P, T, E])
        lsp = sb("lsp", [P, T, E])
        gact = sb("gact", [P, T, E])
        m1 = sb("m1", [P, T])
        p1 = sb("p1", [P, T])
        oh1 = sb("oh1", [P, T, E])
        oh2 = sb("oh2", [P, T, E])
        sel = sb("sel", [P, T, E])
        rest = sb("rest", [P, T, E])
        cfx = sb("cfx", [P, T, 96])
        hs = sb("hs", [P, NB, HT])
        gt = sb("gt", [P, 2, NB + 1, HT])
        yo = sb("yo", [P, 2, TH, P])

        def cut(t, at, n):
            return t[:, at:at + n]

        def tiles(v):
            return v.rearrange("p (t q) -> p t q", q=P)

        assert total >= 4 * L + 2
        gxn, gxT = tiles(cut(fa, 0, L)), tiles(cut(fa, L, L))
        gab, gre = cut(fa, 2 * L, L), cut(fa, 3 * L, L)
        gdl, gsu = cut(fs, 0, L + 1), cut(fs, L + 1, L + 1)
        gw, gd = cut(fs, 2 * L + 2, L), cut(fs, 3 * L + 2, L)
        gs, gv, gh, gy = cut(fv, 0, L), cut(fv, L, L), cut(fv, 2 * L, L), tiles(cut(fv, 3 * L, L))
        gst = sb("gst", [P, T, 6])
        gmv = sb("gmv", [P, T, 2])
        grs = sb("grs", [P, T])
        gbc = sb("gbc", [P, T, 2 * N])
        gbn = sb("gbn", [P, 2, T])
        gan = sb("gan", [P, 1])

        wideg = cut(fs, 0, 2 * TH * E * H).rearrange("p (h t n) -> p h t n", h=2, t=TH)

        def sems(names):
            return [sem(n) for n in names.split()]

        ld_tail, ld_rest, ld_wx, ld_wout, ld_small, ld_bout, ld_ffn1, ld_ffn2, ld_rw = \
            sems("ld_tail ld_rest ld_wx ld_wout ld_small ld_bout ld_ffn1 ld_ffn2 ld_rw")
        stored = sems("stored0 stored1")
        zeroed, consts, wxT_t, wxT_c, wcomb_p, wcomb_c, rwT_p, rwT_c, dwout_c, aneg_c, aval_c, res_init = \
            sems("zeroed consts wxT_t wxT_c wcomb_p wcomb_c rwT_p rwT_c dwout_c aneg_c aval_c res_init")
        t_st, t_mv, t_ve, t_rs, t_xn, t_tp, t_xT, t_z, t_ab, t_ex, t_re, t_ln, t_dl, t_su, t_w = \
            sems("t_st t_mv t_ve t_rs t_xn t_tp t_xT t_z t_ab t_ex t_re t_ln t_dl t_su t_w")
        t_bcp, t_bc, t_gp, t_gm, t_gt, t_g1, t_flag, t_B, t_C, t_v, t_a, t_a0, t_s, t_h, t_hs = \
            sems("t_bcp t_bc t_gp t_gm t_gt t_g1 t_flag t_B t_C t_v t_a t_a0 t_s t_h t_hs")
        t_zc, t_red, t_y, t_yall, t_o, t_res = sems("t_zc t_red t_y t_yall t_o t_res")
        g_st, g_mv, g_ve, g_rs, g_xn, g_tp, g_xT, g_z, g_bcp, g_bc, g_ab, g_ex, g_re, g_ln, g_dl = \
            sems("g_st g_mv g_ve g_rs g_xn g_tp g_xT g_z g_bcp g_bc g_ab g_ex g_re g_ln g_dl")
        g_zero, g_su, g_w, g_col, g_BC, g_a, g_s, g_v, g_h, g_hs, g_zc, g_y, g_o, g_res = \
            sems("g_zero g_su g_w g_col g_BC g_a g_s g_v g_h g_hs g_zc g_y g_o g_res")
        s_st, s_mv, s_ve, s_rs, s_xT, s_x1 = sems("s_st s_mv s_ve s_rs s_xT s_x1")
        s_xn, s_tp, s_o = sems("s_xn0 s_xn1"), sems("s_tp0 s_tp1"), sems("s_o0 s_o1")
        n_st, n_mv, n_ve, n_rs, n_xT = sems("n_st n_mv n_ve n_rs n_xT")
        n_xn, n_tp = sems("n_xn0 n_xn1"), sems("n_tp0 n_tp1")
        r_p, r_lg, r_ab, r_ex, r_ln, r_sp, r_act, r_m1, r_eq1, r_w1, r_p1, r_oh1, r_rest, r_m2 = \
            sems("r_p r_lg r_ab r_ex r_ln r_sp r_act r_m1 r_eq1 r_w1 r_p1 r_oh1 r_rest r_m2")
        r_eq2, r_w2, r_p2, r_oh2, r_sel, r_cf = sems("r_eq2 r_w2 r_p2 r_oh2 r_sel r_cf")
        f_wide, f_up, f_silu, f_cf, f_g, f_out = sems("f_wide f_up f_silu f_cf f_g f_out")
        f_dn = sems("f_dn0 f_dn1")

        waited = sem("waited")

        block = ctx.enter_context(nc.Block())

        x_v = x.rearrange("b (t p) d -> p b t d", p=P)
        out_v = out.rearrange("b (t p) d -> p b t d", p=P)
        GENERAL = 1
        NK = NB + 1

        def col(v):
            return v.rearrange("(p a) -> p a", a=1)

        def row_bc(v):
            return v.rearrange("(a n) -> a n", a=1).to_broadcast([P, v.shape[0]])

        def past(eng, semaphore, count):
            if not (isinstance(count, int) and count <= 0):
                eng.wait_ge(semaphore, count)

        def stop_for(eng, semaphore, count):
            eng.wait_ge(semaphore, count)
            eng.sem_inc(waited, 1)

        def n_tiles(h):
            return TH if h == 0 else TH - TT

        def flat(t, c):
            _, ns, w, _, _ = CLASSES[c]
            return t[:, offs[c]:offs[c] + ns * B * w]

        def wide(t, c):
            _, ns, w, _, _ = CLASSES[c]
            return flat(t, c).rearrange("p (n b w) -> p n b w", n=ns, b=B)

        banks = bank[:, :, :].rearrange("p k n -> p (k n)")

        def psum_class(c, first):
            _, ns, w, _, _ = CLASSES[c]
            return banks[:, 512 * first:512 * first + ns * B * w]

        def two(k):
            return banks[:, 512 * k:512 * (k + 2)]

        @block.sync
        def _(sp):
            for h in range(2):
                sp.sem_inc(stored[h], 16 * FREE)
            for b in range(B):
                sp.dma_start(xa[:, b, T - TT:T, :], x_v[:, b, T - TT:T, :]).then_inc(ld_tail, 16)
            for b in range(B):
                sp.dma_start(xa[:, b, 0:T - TT, :], x_v[:, b, 0:T - TT, :]).then_inc(ld_rest, 16)
            with sp.Fori(0, B) as b:
                for h in range(2):
                    sp.wait_ge(f_out, 2 * b + h + 1 + FREE)
                    sp.dma_start(out_v[:, b, TH * h:TH * h + TH, :], yo[:, h, :, :]).then_inc(stored[h], 16)
            for h in range(2):
                sp.wait_ge(stored[h], 16 * B + 16 * FREE)

        @block.gpsimd
        def _(pool):
            pool.memset(ident[:, :], 0.0).then_inc(zeroed, 1)
            pool.wait_ge(zeroed, 1)
            pool.affine_select(out=ident[:, :], in_=ident[:, :], compare_op=ALU.not_equal, fill=1.0,
                               base=0, pattern=[[-1, P]], channel_multiplier=1).then_inc(consts, 1)
            pool.memset(epsv[:, :], LN_EPS).then_inc(consts, 1)
            pool.memset(mhalf[:, :], -0.5).then_inc(consts, 1)
            pool.memset(phalf[:, :], 0.5).then_inc(consts, 1)
            pool.memset(logt[:, :], LOG_TINY).then_inc(consts, 1)
            pool.memset(mask[:, :], 1.0).then_inc(zeroed, 1)
            pool.memset(tdl[:, :, TAIL:SEG], 0.0).then_inc(consts, 1)
            pool.wait_ge(zeroed, 2)
            pool.memset(mask[:, TAIL::SEG], 0.0).then_inc(consts, 1)
            for e in range(E):
                pool.memset(ramp[:, e:e + 1], float(E - e)).then_inc(consts, 1)
            pool.memset(cfx[:, :, :], 0.0).then_inc(zeroed, 1)
            pool.wait_ge(zeroed, 3)
            pool.memset(cfx[:, :, H + E:KX], 1.0).then_inc(consts, 1)

            def inv_sqrt(rs, mv, n, mv_ready, sum_ready, ready, u):
                pool.wait_ge(mv_ready, u + 1)
                pool.tensor_tensor(rs, mv, epsv[:, 0:n], ALU.add).then_inc(sum_ready, 1)
                pool.wait_ge(sum_ready, u + 1)
                pool.tensor_tensor(rs, rs, mhalf[:, 0:n], ALU.pow).then_inc(ready, 1)

            pool.wait_ge(consts, 3)
            inv_sqrt(trs[:, :], tmv[:, :, 1], TB, t_mv, t_ve, t_rs, 0)
            pool.wait_ge(ld_bout, 16)
            pool.wait_ge(ld_tail, 16 * B)
            for b in range(B):
                pool.tensor_tensor(ra[:, b, T - TT:T, :], xa[:, b, T - TT:T, :],
                                   bout[:, :].unsqueeze(1).to_broadcast([P, TT, P]),
                                   ALU.add).then_inc(res_init, 1)
            pool.wait_ge(t_dl, 1)
            pool.wait_ge(t_xT, 2)
            pool.tensor_tensor(tw[:, :, :], tdl[:, :, 0:TAIL],
                               txT[:, :, :].rearrange("p (b s) q -> p b (s q)", b=B),
                               ALU.mult).then_inc(t_w, 1)
            for c, (_, ns, w, _, _) in enumerate(CLASSES):
                pool.wait_ge(t_a, sum(q[1] for q in CLASSES[:c + 1]))
                pool.memset(flat(fa, c)[:, 0::w], 0.0).then_inc(t_a0, 1)
            pool.wait_ge(ld_rest, 16 * B)
            for b in range(B):
                pool.tensor_tensor(ra[:, b, 0:T - TT, :], xa[:, b, 0:T - TT, :],
                                   bout[:, :].unsqueeze(1).to_broadcast([P, T - TT, P]),
                                   ALU.add).then_inc(res_init, 1)

            pool.wait_ge(t_flag, 1)
            with pool.If(pool.value_load(flag[0:1, 0:1], min_val=0, max_val=1) == GENERAL):
                with pool.Fori(0, B) as b:
                    inv_sqrt(grs[:, :], gmv[:, :, 1], T, g_mv, g_ve, g_rs, b)

            with pool.Fori(0, B) as b:
                for h in range(2):
                    n, u = n_tiles(h), 2 * b + h
                    inv_sqrt(rs1[:, h, 0:n], mv1[:, h, 0:n, 1], n, s_mv, s_ve, s_rs, u)
                    inv_sqrt(rs2[:, h, :], mv2[:, h, :, 1], TH, n_mv, n_ve, n_rs, u)
                pool.wait_ge(r_sp, b + 1)
                pool.tensor_tensor(gact[:, :, :].rearrange("p t e -> p (t e)"),
                                   lsp[:, :, :].rearrange("p t e -> p (t e)"),
                                   phalf[:, :], ALU.pow).then_inc(r_act, 1)
                pool.wait_ge(r_cf, b + 1)
                for h in range(2):
                    stop_for(pool, f_dn[h], b + FREE)
                    pool.tensor_copy(wideg[:, h, :, :].rearrange("p t (e h) -> p t e h", e=E),
                                     cfx[:, TH * h:TH * h + TH, H:H + E].unsqueeze(3)
                                     .to_broadcast([P, TH, E, H])).then_inc(f_wide, 1)

        @block.scalar
        def _(act):
            act.sem_inc(f_silu, FREE)
            act.dma_start(wx[:, :], W_x).then_inc(ld_wx, 16)
            act.dma_start(wdt[:, :], W_dt).then_inc(ld_wx, 16)
            act.dma_start(alog[:, :], A_log).then_inc(ld_small, 16)
            act.dma_start(bdt[:, :], col(b_dt)).then_inc(ld_small, 16)
            act.dma_start(dcol[:, :], col(D)).then_inc(ld_wout, 16)
            act.dma_start(wout[:, :], W_out).then_inc(ld_wout, 16)
            act.dma_start(bout[:, :], row_bc(b_out)).then_inc(ld_bout, 16)
            act.dma_start(rw[:, :], routing_W).then_inc(ld_rw, 16)
            act.dma_start(ebias[:, :], row_bc(expert_bias)).then_inc(ld_rw, 16)
            act.dma_start(w1[:, 0:E * H].rearrange("p (e h) -> p e h", e=E),
                          rW1.rearrange("e d h -> d e h")).then_inc(ld_ffn1, 16)
            act.dma_start(w1[:, E * H:(E + 1) * H], sW1).then_inc(ld_ffn1, 16)
            for k in range(NB):
                act.dma_start(b1[:, k:k + 1], rb1[EB * k:EB * k + EB, :].rearrange("e (h a) -> (e h) a", a=1))\
                   .then_inc(ld_ffn1, 16)
            act.dma_start(b1[0:H, NB:NK], col(sb1)).then_inc(ld_ffn1, 16)
            for k in range(NB):
                act.dma_start(w2[:, k, :], rW2[EB * k:EB * k + EB, :, :].rearrange("e h d -> (e h) d"))\
                   .then_inc(ld_ffn2, 16)
            act.dma_start(w2[0:H, NB, :], sW2).then_inc(ld_ffn2, 16)
            act.dma_start(w2[H:H + E, NB, :], rb2).then_inc(ld_ffn2, 16)
            act.dma_start(w2[H + E:KX, NB, :], sb2.rearrange("(a d) -> a d", a=1)).then_inc(ld_ffn2, 16)

            act.wait_ge(ld_small, 32)
            act.activation(aneg[:, :], alog[:, :], ACT.Exp).then_inc(aneg_c, 1)
            act.wait_ge(aneg_c, 1)
            act.mul(aval[:, :], aneg[:, :], -1.0).then_inc(aval_c, 1)
            act.wait_ge(wxT_t, 1)
            act.copy(wxT[:, :], bank[0:R, 7, 0:P]).then_inc(wxT_c, 1)
            act.wait_ge(rwT_p, 1)
            act.copy(rwT[:, :], bank[:, 6, 0:E]).then_inc(rwT_c, 1)
            act.wait_ge(wcomb_p, 1)
            act.copy(wcomb[:, :], bank[:, 5, 0:P]).then_inc(wcomb_c, 1)
            for k in range(2):
                act.wait_ge(t_tp, k + 1)
                act.copy(txT[:, TB // 2 * k:TB // 2 * (k + 1), :].rearrange("p t q -> p (t q)"),
                         bank[:, k, :]).then_inc(t_xT, 1)
            act.wait_ge(t_z, 1)
            act.activation(tre[:, :, :].rearrange("p b w -> p (b w)"), two(2), ACT.Relu,
                           bias=bdt[:, :]).then_inc(t_re, 1)
            act.activation(tab[:, :, :].rearrange("p b w -> p (b w)"), two(2), ACT.Abs,
                           bias=bdt[:, :]).then_inc(t_ab, 1)
            act.wait_ge(t_ab, 1)
            act.activation(tex[:, :, :], tab[:, :, :], ACT.Exp, scale=-1.0).then_inc(t_ex, 1)
            act.wait_ge(t_ex, 1)
            act.activation(tab[:, :, :], tex[:, :, :], ACT.Ln, bias=1.0).then_inc(t_ln, 1)
            act.wait_ge(t_bcp, 1)
            act.copy(tbc[:, :, :].rearrange("p t n -> p (t n)"), bank[:, 4, 0:TB * 2 * N]).then_inc(t_bc, 1)
            act.wait_ge(t_dl, 1)
            act.wait_ge(aval_c, 1)
            for c, (k0, ns, w, _, _) in enumerate(CLASSES):
                for n in range(ns):
                    act.activation(wide(fa, c)[:, n], tdl[:, :, TAIL - w:TAIL], ACT.Exp,
                                   scale=aval[:, k0 + n:k0 + n + 1]).then_inc(t_a, 1)
            act.wait_ge(t_su, 1)
            act.wait_ge(consts, 5)
            for c, (k0, ns, w, _, _) in enumerate(CLASSES):
                for n in range(ns):
                    act.activation(wide(fs, c)[:, n], tsu[:, :, SEG - w:SEG], ACT.Sigmoid,
                                   scale=aval[:, k0 + n:k0 + n + 1], bias=logt[:, :]).then_inc(t_s, 1)

            act.wait_ge(t_flag, 1)
            with act.If(act.value_load(flag[0:1, 0:1], min_val=0, max_val=1) == GENERAL):
                with act.Fori(0, B) as b:
                    act.wait_ge(g_tp, b + 1)
                    act.copy(gxT[:, :, :].rearrange("p t q -> p (t q)"), two(0)).then_inc(g_xT, 1)
                    act.wait_ge(g_z, b + 1)
                    act.activation(gre[:, :], two(2), ACT.Relu, bias=bdt[:, :]).then_inc(g_re, 1)
                    act.activation(gab[:, :], two(2), ACT.Abs, bias=bdt[:, :]).then_inc(g_ab, 1)
                    act.wait_ge(g_ab, b + 1)
                    act.activation(gd[:, :], gab[:, :], ACT.Exp, scale=-1.0).then_inc(g_ex, 1)
                    act.wait_ge(g_ex, b + 1)
                    act.activation(gab[:, :], gd[:, :], ACT.Ln, bias=1.0).then_inc(g_ln, 1)
                    act.wait_ge(g_bcp, b + 1)
                    act.copy(gbc[:, :, :].rearrange("p t n -> p (t n)"), bank[:, 4, 0:T * 2 * N]).then_inc(g_bc, 1)
                    stop_for(act, g_su, b + 1)
                    with act.Fori(0, N) as n:
                        i = N * b + n
                        act.wait_ge(g_col, 3 * i + 3)
                        act.wait_ge(g_h, i + FREE)
                        act.activation(gd[:, :], gdl[:, 0:L], ACT.Exp, scale=gan[:, :]).then_inc(g_a, 1)
                        act.wait_ge(g_hs, i + FREE)
                        act.activation(gs[:, :], gsu[:, 1:L + 1], ACT.Sigmoid, scale=gan[:, :],
                                       bias=logt[:, :]).then_inc(g_s, 1)

            def evac1(b, h):
                n = n_tiles(h)
                act.wait_ge(s_tp[h], b + 1)
                past(act, s_o[h], b)
                act.copy(xT1[:, h, 0:n, :].rearrange("p t q -> p (t q)"), bank[:, 0, 0:n * P]).then_inc(s_xT, 1)

            def evac2(b, h, last):
                act.wait_ge(n_tp[h], b + 1)
                if last is not None:
                    act.wait_ge(f_up, NK * (2 * last + h + 1))
                past(act, r_p, b)
                act.copy(xT2[:, h, :], bank[:, 0, :]).then_inc(n_xT, 1)

            def softplus(b):
                act.wait_ge(r_lg, b + 1)
                act.activation(lga[:, :, :], lg[:, :, :], ACT.Abs).then_inc(r_ab, 1)
                act.wait_ge(r_ab, b + 1)
                act.activation(lge[:, :, :], lga[:, :, :], ACT.Exp, scale=-1.0).then_inc(r_ex, 1)
                act.wait_ge(r_ex, b + 1)
                act.activation(lga[:, :, :], lge[:, :, :], ACT.Ln, bias=1.0).then_inc(r_ln, 1)

            def silu(b, h):
                u = 2 * b + h
                for k in range(NK):
                    j = NK * u + k
                    act.wait_ge(f_up, j + 1)
                    src = bank[:, 2 + (NK * h + k) % 2, :]
                    if k < NB:
                        past(act, f_g, NK * u + FREE)
                        act.activation(hs[:, k, :], src, ACT.Silu, bias=b1[:, k:k + 1]).then_inc(f_silu, 1)
                    else:
                        past(act, f_dn[h], b + FREE)
                        act.activation(gt[0:H, h, k, :], src[0:H, :], ACT.Silu,
                                       bias=b1[0:H, k:k + 1]).then_inc(f_silu, 1)

            act.wait_ge(ld_ffn1, 16 * (NB + 3))
            for h in range(2):
                evac1(0, h)
                evac2(0, h, None)
            softplus(0)
            with act.Fori(0, B - 1) as b:
                for h in range(2):
                    silu(b, h)
                    evac1(b + 1, h)
                    evac2(b + 1, h, b)
                softplus(b + 1)
            for h in range(2):
                silu(B - 1, h)

        @block.tensor
        def _(pe):
            for h in range(2):
                pe.sem_inc(f_dn[h], FREE)
            pe.wait_ge(consts, 1)
            pe.wait_ge(ld_wx, 32)
            pe.transpose(bank[0:R, 7, 0:P], wx[:, 0:R], ident[:, :]).then_inc(wxT_t, 1)
            pe.wait_ge(ld_rw, 32)
            pe.transpose(bank[:, 6, 0:E], rw[:, :], ident[0:E, 0:E]).then_inc(rwT_p, 1)
            pe.wait_ge(wxT_c, 1)
            pe.matmul(bank[:, 5, 0:P], wxT[:, :], wdt[:, :], start=True, stop=True).then_inc(wcomb_p, 1)
            for k in range(2):
                for j in range(TB // 2):
                    q = TB // 2 * k + j
                    pe.wait_ge(t_xn, q + 1)
                    mm = pe.transpose(bank[:, k, P * j:P * j + P], txn[:, q, :], ident[:, :])
                mm.then_inc(t_tp, 1)
            pe.wait_ge(wcomb_c, 1)
            for k in range(2):
                pe.wait_ge(t_xT, k + 1)
                mm = pe.matmul(bank[:, 2 + k, :], wcomb[:, :],
                               txT[:, TB // 2 * k:TB // 2 * (k + 1), :].rearrange("p t q -> p (t q)"),
                               start=True, stop=True)
            mm.then_inc(t_z, 1)
            for q in range(TB):
                mm = pe.matmul(bank[:, 4, 2 * N * q:2 * N * (q + 1)], txT[:, q, :], wx[:, R:R + 2 * N],
                               start=True, stop=True)
            mm.then_inc(t_bcp, 1)
            pe.wait_ge(t_gm, 1)
            pe.transpose(bank[0:1, 5, 0:P], gmax[:, :], ident[:, :]).then_inc(t_gt, 1)

            def spread(c, first, column):
                k0, ns, w, _, _ = CLASSES[c]
                for n in range(ns):
                    for b in range(B):
                        at = 512 * first + (n * B + b) * w
                        for s in range(max(1, w // P)):
                            rows = min(w, P)
                            q = TT * b + TT - max(1, w // P) + s
                            lo = P - rows
                            src = tbc[lo:P, q, column + k0 + n:column + k0 + n + 1].to_broadcast([rows, P])
                            mm = pe.transpose(banks[:, at + s * P:at + s * P + rows], src,
                                              ident[lo:P, lo:P])
                return mm

            pe.wait_ge(t_bc, 1)
            pe.wait_ge(t_re, 1)
            pe.wait_ge(t_ab, 1)
            pe.wait_ge(t_g1, 1)
            pe.wait_ge(rwT_c, 1)
            for c, (_, _, _, first, _) in enumerate(CLASSES):
                if c == len(CLASSES) - 1:
                    pe.wait_ge(t_v, 1)
                spread(c, first, 0).then_inc(t_B, 1)
            for c in C_ORDER:
                free = {0: 2, 1: 3, 2: 4, 4: 4, 3: 5}[c]
                pe.wait_ge(t_v, free)
                if c == 3:
                    pe.wait_ge(t_zc, 1)
                spread(c, CLASSES[c][4], N).then_inc(t_C, 1)

            pe.wait_ge(t_flag, 1)
            with pe.If(pe.value_load(flag[0:1, 0:1], min_val=0, max_val=1) == GENERAL):
                with pe.Fori(0, B) as b:
                    pe.wait_ge(g_xn, b + 1)
                    for t in range(T):
                        mm = pe.transpose(banks[:, P * t:P * t + P], gxn[:, t, :], ident[:, :])
                    mm.then_inc(g_tp, 1)
                    pe.wait_ge(g_xT, b + 1)
                    for k in range(2):
                        mm = pe.matmul(bank[:, 2 + k, :], wcomb[:, :],
                                       gxT[:, TH * k:TH * (k + 1), :].rearrange("p t q -> p (t q)"),
                                       start=True, stop=True)
                    mm.then_inc(g_z, 1)
                    for t in range(T):
                        mm = pe.matmul(bank[:, 4, 2 * N * t:2 * N * (t + 1)], gxT[:, t, :],
                                       wx[:, R:R + 2 * N], start=True, stop=True)
                    mm.then_inc(g_bcp, 1)
                    stop_for(pe, g_dl, b + 1)
                    with pe.Fori(0, N) as n:
                        i = N * b + n
                        pe.wait_ge(g_col, 3 * i + 3)
                        pe.wait_ge(g_zc, i + FREE)
                        for s in range(2):
                            for t in range(T):
                                mm = pe.transpose(banks[:, 1024 * (1 + s) + P * t:1024 * (1 + s) + P * t + P],
                                                  gbn[:, s, t:t + 1].to_broadcast([P, P]), ident[:, :])
                        mm.then_inc(g_BC, 1)
                    pe.wait_ge(g_y, N * b + N)
                    for t in range(T):
                        mm = pe.matmul(banks[:, 3072 + P * t:3072 + P * t + P], gy[:, t, :], wout[:, :],
                                       start=True, stop=True)
                    mm.then_inc(g_o, 1)

            pe.wait_ge(t_yall, 1)
            pe.wait_ge(dwout_c, 1)
            for q in range(TB):
                dst = banks[:, 1024 + P * q:1024 + P * q + P]
                pe.matmul(dst, txT[:, q, :], dwout[:, :], start=True, stop=False)
                mm = pe.matmul(dst, yT[:, q // TT, P * (q % TT):P * (q % TT) + P], wout[:, :],
                               start=False, stop=True)
            mm.then_inc(t_o, 1)
            pe.wait_ge(t_res, 1)

            def attn_out(b, h):
                n, u = n_tiles(h), 2 * b + h
                pe.wait_ge(s_xn[h], b + 1)
                past(pe, n_xT, u)
                for t in range(n):
                    mm = pe.transpose(bank[:, 0, P * t:P * t + P], xn1[:, h, t, :], ident[:, :])
                mm.then_inc(s_tp[h], 1)
                pe.wait_ge(s_xT, u + 1)
                past(pe, s_x1, u)
                for t in range(n):
                    mm = pe.matmul(bank[:, 1, P * t:P * t + P], xT1[:, h, t, :], dwout[:, :],
                                   start=True, stop=True)
                mm.then_inc(s_o[h], 1)

            def turn2(b, h):
                pe.wait_ge(n_xn[h], b + 1)
                pe.wait_ge(s_xT, 2 * b + h + 1)
                for t in range(TH):
                    mm = pe.transpose(bank[:, 0, P * t:P * t + P], xn2[:, h, t, :], ident[:, :])
                mm.then_inc(n_tp[h], 1)

            def router(b):
                pe.wait_ge(n_xT, 2 * b + 2)
                past(pe, r_lg, b)
                for t in range(T):
                    mm = pe.matmul(bank[:, 7, E * t:E * t + E],
                                   xT2[:, t // TH, P * (t % TH):P * (t % TH) + P], rwT[:, :],
                                   start=True, stop=True)
                mm.then_inc(r_p, 1)

            def up(b, h):
                u = 2 * b + h
                pe.wait_ge(n_xT, u + 1)
                for k in range(NK):
                    j = NK * u + k
                    odd = (NK * h + k) % 2
                    m = P if k < NB else H
                    past(pe, f_silu, NK * u + max(k - 1, 0) + FREE)
                    pe.matmul(bank[0:m, 2 + odd, :], w1[:, P * k:P * k + m], xT2[:, h, :],
                              start=True, stop=True).then_inc(f_up, 1)
                    if k == 0:
                        pe.wait_ge(f_wide, u + 1)
                    past(pe, f_g, NK * u + max(k - 1, 0) + FREE)
                    for t in range(TH):
                        g = cfx[:, TH * h + t, :]
                        if k < NB:
                            mm = pe.transpose(bank[:, 4 + odd, P * t:P * t + P],
                                              wideg[:, h, t, P * k:P * k + P], ident[:, :])
                        else:
                            mm = pe.transpose(bank[0:96, 4 + odd, P * t:P * t + P], g, ident[:, :])
                    mm.then_inc(f_cf, 1)

            def down(b, h):
                u = 2 * b + h
                pe.wait_ge(f_g, NK * u + NK + FREE)
                pe.wait_ge(f_silu, NK * u + NK + FREE)
                past(pe, f_out, u + FREE)
                for t in range(TH):
                    for k in range(NK):
                        rows = P if k < NB else KX
                        mm = pe.matmul(bank[:, 6, P * t:P * t + P], gt[0:rows, h, k, P * t:P * t + P],
                                       w2[0:rows, k, :], start=(k == 0), stop=(k == NK - 1))
                mm.then_inc(f_dn[h], 1)

            for h in range(2):
                attn_out(0, h)
                turn2(0, h)
            router(0)
            pe.wait_ge(ld_ffn1, 16 * (NB + 3))
            pe.wait_ge(ld_ffn2, 16 * (NB + 3))
            with pe.Fori(0, B - 1) as b:
                for h in range(2):
                    up(b, h)
                    attn_out(b + 1, h)
                    down(b, h)
                    turn2(b + 1, h)
                router(b + 1)
            for h in range(2):
                up(B - 1, h)
                down(B - 1, h)

        @block.vector
        def _(dve):
            for used in (f_g, f_out, g_h, g_hs, g_zc):
                dve.sem_inc(used, FREE)
            for b in range(B):
                for s in range(TT):
                    q = TT * b + s
                    if s == 0:
                        dve.wait_ge(ld_tail, 16 * B)
                    dve.bn_stats(tst[:, q, :], xa[:, b, T - TT + s, :]).then_inc(t_st, 1)
            for q in range(TB):
                dve.wait_ge(t_st, q + 1)
                mv = dve.bn_aggr(tmv[:, q, :], tst[:, q, :])
            mv.then_inc(t_mv, 1)
            dve.wait_ge(ld_wout, 32)
            dve.tensor_scalar(dwout[:, :], wout[:, :], dcol[:, :], None, ALU.mult).then_inc(dwout_c, 1)
            dve.wait_ge(t_rs, 1)
            for q in range(TB):
                dve.tensor_scalar(txn[:, q, :], xa[:, q // TT, T - TT + q % TT, :], tmv[:, q, 0:1],
                                  trs[:, q:q + 1], ALU.subtract, ALU.mult).then_inc(t_xn, 1)
            dve.wait_ge(t_ln, 1)
            dve.wait_ge(t_re, 1)
            dve.tensor_tensor(tdl[:, :, 0:TAIL], tre[:, :, :], tab[:, :, :], ALU.add).then_inc(t_dl, 1)
            dve.wait_ge(consts, 7)
            dve.wait_ge(t_dl, 1)
            dve.tensor_tensor_scan(tsu[:, :, :].rearrange("p b w -> p (b w)")[:, ::-1], mask[:, ::-1],
                                   tdl[:, :, :].rearrange("p b w -> p (b w)")[:, ::-1], 0.0,
                                   ALU.mult, ALU.add).then_inc(t_su, 1)
            dve.wait_ge(t_su, 1)
            dve.wait_ge(aval_c, 1)
            for c, (k0, ns, w, _, _) in enumerate(CLASSES):
                gp = dve.tensor_tensor(gprod[:, k0:k0 + ns, :],
                                       aval[:, k0:k0 + ns].unsqueeze(2).to_broadcast([P, ns, B]),
                                       tsu[:, :, TAIL - w].unsqueeze(1).to_broadcast([P, ns, B]), ALU.mult)
            gp.then_inc(t_gp, 1)
            dve.wait_ge(t_gp, 1)
            dve.tensor_reduce(gmax[:, :], gprod[:, :, :].rearrange("p n b -> p (n b)"), AX.X, ALU.max)\
               .then_inc(t_gm, 1)
            dve.wait_ge(t_gt, 1)
            dve.tensor_reduce(gmx1[:, :], bank[0:1, 5, 0:P], AX.X, ALU.max).then_inc(t_g1, 1)
            dve.wait_ge(t_g1, 1)
            dve.tensor_scalar(flag[:, :], gmx1[:, :], UNDERFLOW, None, ALU.is_ge).then_inc(t_flag, 1)

            dve.wait_ge(t_w, 1)
            for c, (_, ns, w, first, _) in enumerate(CLASSES):
                dve.wait_ge(t_B, c + 1)
                dve.tensor_tensor(wide(fv, c), psum_class(c, first).rearrange("p (n b w) -> p n b w", n=ns, b=B),
                                  tw[:, :, TAIL - w:TAIL].unsqueeze(1).to_broadcast([P, ns, B, w]),
                                  ALU.mult).then_inc(t_v, 1)
            for c in range(len(CLASSES)):
                dve.wait_ge(t_v, c + 1)
                dve.wait_ge(t_a0, c + 1)
                dve.tensor_tensor_scan(flat(fv, c), flat(fa, c), flat(fv, c), 0.0, ALU.mult, ALU.add)\
                   .then_inc(t_h, 1)
            for i, c in enumerate(C_ORDER):
                dve.wait_ge(t_h, len(CLASSES) if i else 1)
                dve.wait_ge(t_s, sum(q[1] for q in CLASSES[:c + 1]))
                dve.tensor_tensor(flat(fa, c), flat(fv, c), flat(fs, c), ALU.mult).then_inc(t_hs, 1)
                dve.wait_ge(t_C, i + 1)
                dve.wait_ge(t_hs, i + 1)
                dve.tensor_tensor(flat(fv, c), flat(fa, c), psum_class(c, CLASSES[c][4]), ALU.mult)\
                   .then_inc(t_zc, 1)
            dve.wait_ge(t_zc, len(CLASSES))
            for i, c in enumerate((1, 2, 3)):
                _, ns, w, _, _ = CLASSES[c]
                dve.tensor_reduce(red[:, i, 0:B * w], wide(fv, c).rearrange("p n b w -> p (b w) n"),
                                  AX.X, ALU.add).then_inc(t_red, 1)
            dve.tensor_copy(yT[:, :, :], wide(fv, 0)[:, 0]).then_inc(t_y, 1)
            parts = [(red[:, i, 0:B * CLASSES[c][2]].rearrange("p (b w) -> p b w", b=B), CLASSES[c][2])
                     for i, c in enumerate((1, 2, 3))] + [(wide(fv, 4)[:, 0], CLASSES[4][2])]
            dve.wait_ge(t_red, 3)
            for i, (part, w) in enumerate(parts):
                dve.wait_ge(t_y, i + 1)
                dve.tensor_tensor(yT[:, :, TAIL - w:TAIL], yT[:, :, TAIL - w:TAIL], part, ALU.add)\
                   .then_inc(t_y, 1)
            dve.wait_ge(t_y, len(parts) + 1)
            dve.wait_ge(res_init, 2 * B)
            dve.wait_ge(ld_rest, 16 * B)

            dve.wait_ge(t_flag, 1)
            with dve.If(dve.value_load(flag[0:1, 0:1], min_val=0, max_val=1) == GENERAL):
                dve.memset(gdl[:, L:L + 1], 0.0).then_inc(g_zero, 1)
                with dve.Fori(0, B) as b:
                    for t in range(T):
                        dve.bn_stats(gst[:, t, :], xa[:, b, t, :]).then_inc(g_st, 1)
                    stop_for(dve, g_st, T * b + T)
                    for t in range(T):
                        mv = dve.bn_aggr(gmv[:, t, :], gst[:, t, :])
                    mv.then_inc(g_mv, 1)
                    dve.wait_ge(g_rs, b + 1)
                    for t in range(T):
                        xn = dve.tensor_scalar(gxn[:, t, :], xa[:, b, t, :], gmv[:, t, 0:1],
                                               grs[:, t:t + 1], ALU.subtract, ALU.mult)
                    xn.then_inc(g_xn, 1)
                    dve.wait_ge(g_ln, b + 1)
                    dve.wait_ge(g_re, b + 1)
                    dve.tensor_tensor(gdl[:, 0:L], gre[:, :], gab[:, :], ALU.add).then_inc(g_dl, 1)
                    dve.wait_ge(g_dl, b + 1)
                    dve.wait_ge(g_zero, b + 1)
                    dve.tensor_tensor_scan(gsu[:, ::-1], mask[:, 0:1].to_broadcast([P, L + 1]),
                                           gdl[:, ::-1], 0.0, ALU.mult, ALU.add).then_inc(g_su, 1)
                    dve.tensor_tensor(gw[:, :], gdl[:, 0:L], gxT[:, :, :].rearrange("p t q -> p (t q)"),
                                      ALU.mult).then_inc(g_w, 1)
                    dve.memset(gy[:, :, :], 0.0).then_inc(g_zero, 1)
                    dve.wait_ge(g_zero, b + 2)
                    dve.wait_ge(g_bc, b + 1)
                    stop_for(dve, g_w, b + 1)
                    with dve.Fori(0, N) as n:
                        i = N * b + n
                        dve.tensor_copy(gbn[:, 0, :], gbc[:, :, n]).then_inc(g_col, 1)
                        dve.tensor_copy(gbn[:, 1, :], gbc[:, :, N + n]).then_inc(g_col, 1)
                        dve.tensor_copy(gan[:, :], aval[:, bass.ds(n, 1)]).then_inc(g_col, 1)
                        dve.wait_ge(g_BC, i + 1)
                        dve.tensor_tensor(gv[:, :], gw[:, :], two(2), ALU.mult).then_inc(g_v, 1)
                        dve.wait_ge(g_v, i + 1)
                        dve.wait_ge(g_a, i + 1)
                        dve.tensor_tensor_scan(gh[:, :], gd[:, :], gv[:, :], 0.0, ALU.mult, ALU.add)\
                           .then_inc(g_h, 1)
                        dve.wait_ge(g_h, i + 1 + FREE)
                        dve.wait_ge(g_s, i + 1)
                        dve.tensor_tensor(gv[:, :], gh[:, :], gs[:, :], ALU.mult).then_inc(g_hs, 1)
                        dve.wait_ge(g_hs, i + 1 + FREE)
                        dve.tensor_tensor(gh[:, :], gv[:, :], two(4), ALU.mult).then_inc(g_zc, 1)
                        dve.wait_ge(g_zc, i + 1 + FREE)
                        dve.tensor_tensor(gy[:, :, :].rearrange("p t q -> p (t q)"),
                                          gy[:, :, :].rearrange("p t q -> p (t q)"), gh[:, :],
                                          ALU.add).then_inc(g_y, 1)
                        dve.wait_ge(g_y, i + 1)
                    dve.wait_ge(g_o, b + 1)
                    dve.tensor_tensor(ra[:, b, 0:T - TT, :].rearrange("p t q -> p (t q)"),
                                      ra[:, b, 0:T - TT, :].rearrange("p t q -> p (t q)"),
                                      banks[:, 3072:3072 + P * (T - TT)], ALU.add).then_inc(g_res, 1)
                    dve.tensor_copy(yT[:, b, :], gy[:, T - TT:T, :].rearrange("p t q -> p (t q)"))\
                       .then_inc(g_res, 1)
                    stop_for(dve, g_res, 2 * b + 2)
            dve.sem_inc(t_yall, 1)

            dve.wait_ge(t_o, 1)
            for b in range(B):
                r = dve.tensor_tensor(ra[:, b, T - TT:T, :].rearrange("p t q -> p (t q)"),
                                      ra[:, b, T - TT:T, :].rearrange("p t q -> p (t q)"),
                                      banks[:, 1024 + TAIL * b:1024 + TAIL * (b + 1)], ALU.add)
            r.then_inc(t_res, 1)
            dve.wait_ge(t_res, 1)

            def norm1(b, h):
                n, u = n_tiles(h), 2 * b + h
                for t in range(n):
                    st = dve.bn_stats(st1[:, h, t, :], xa[:, b, TH * h + t, :])
                st.then_inc(s_st, 1)
                stop_for(dve, s_st, u + 1)
                for t in range(n):
                    mv = dve.bn_aggr(mv1[:, h, t, :], st1[:, h, t, :])
                mv.then_inc(s_mv, 1)
                dve.wait_ge(s_rs, u + 1)
                past(dve, s_tp[h], b)
                for t in range(n):
                    xn = dve.tensor_scalar(xn1[:, h, t, :], xa[:, b, TH * h + t, :], mv1[:, h, t, 0:1],
                                           rs1[:, h, t:t + 1], ALU.subtract, ALU.mult)
                xn.then_inc(s_xn[h], 1)

            def residual1(b, h):
                n, u = n_tiles(h), 2 * b + h
                dve.wait_ge(s_o[h], b + 1)
                r = ra[:, b, TH * h:TH * h + n, :].rearrange("p t q -> p (t q)")
                dve.tensor_tensor(r, r, bank[:, 1, 0:n * P], ALU.add).then_inc(s_x1, 1)
                stop_for(dve, s_x1, u + 1)

            def norm2(b, h):
                u = 2 * b + h
                for t in range(TH):
                    st = dve.bn_stats(st2[:, h, t, :], ra[:, b, TH * h + t, :])
                st.then_inc(n_st, 1)
                stop_for(dve, n_st, u + 1)
                for t in range(TH):
                    mv = dve.bn_aggr(mv2[:, h, t, :], st2[:, h, t, :])
                mv.then_inc(n_mv, 1)
                dve.wait_ge(n_rs, u + 1)
                past(dve, n_tp[h], b)
                for t in range(TH):
                    xn = dve.tensor_scalar(xn2[:, h, t, :], ra[:, b, TH * h + t, :], mv2[:, h, t, 0:1],
                                           rs2[:, h, t:t + 1], ALU.subtract, ALU.mult)
                xn.then_inc(n_xn[h], 1)

            def over_experts(t):
                return t[:, :].unsqueeze(2).to_broadcast([P, T, E])

            def choose(b):
                v = b + 1
                dve.wait_ge(r_p, v)
                dve.tensor_tensor(lg[:, :, :], bank[:, 7, 0:T * E].rearrange("p (t e) -> p t e", e=E),
                                  ebias[:, :].unsqueeze(1).to_broadcast([P, T, E]), ALU.add).then_inc(r_lg, 1)
                dve.wait_ge(r_ln, v)
                dve.scalar_tensor_tensor(out=lsp[:, :, :], in0=lg[:, :, :], scalar=0.0, in1=lga[:, :, :],
                                         op0=ALU.max, op1=ALU.add).then_inc(r_sp, 1)
                ramps = ramp[:, :].unsqueeze(1).to_broadcast([P, T, E])
                dve.wait_ge(r_act, v)
                dve.tensor_reduce(m1[:, :], gact[:, :, :], AX.X, ALU.max).then_inc(r_m1, 1)
                dve.wait_ge(r_m1, v)
                dve.tensor_tensor(oh1[:, :, :], gact[:, :, :], over_experts(m1), ALU.is_equal).then_inc(r_eq1, 1)
                dve.wait_ge(r_eq1, v)
                dve.tensor_tensor(oh2[:, :, :], oh1[:, :, :], ramps, ALU.mult).then_inc(r_w1, 1)
                dve.wait_ge(r_w1, v)
                dve.tensor_reduce(p1[:, :], oh2[:, :, :], AX.X, ALU.max).then_inc(r_p1, 1)
                dve.wait_ge(r_p1, v)
                dve.tensor_tensor(oh1[:, :, :], ramps, over_experts(p1), ALU.is_equal).then_inc(r_oh1, 1)
                dve.wait_ge(r_oh1, v)
                dve.scalar_tensor_tensor(out=rest[:, :, :], in0=oh1[:, :, :], scalar=TIE_DROP,
                                         in1=gact[:, :, :], op0=ALU.mult, op1=ALU.add).then_inc(r_rest, 1)
                dve.wait_ge(r_rest, v)
                dve.tensor_reduce(m1[:, :], rest[:, :, :], AX.X, ALU.max).then_inc(r_m2, 1)
                dve.wait_ge(r_m2, v)
                dve.tensor_tensor(oh2[:, :, :], rest[:, :, :], over_experts(m1), ALU.is_equal).then_inc(r_eq2, 1)
                dve.wait_ge(r_eq2, v)
                dve.tensor_tensor(rest[:, :, :], oh2[:, :, :], ramps, ALU.mult).then_inc(r_w2, 1)
                dve.wait_ge(r_w2, v)
                dve.tensor_reduce(p1[:, :], rest[:, :, :], AX.X, ALU.max).then_inc(r_p2, 1)
                dve.wait_ge(r_p2, v)
                dve.tensor_tensor(oh2[:, :, :], ramps, over_experts(p1), ALU.is_equal).then_inc(r_oh2, 1)
                dve.wait_ge(r_oh2, v)
                dve.tensor_tensor(sel[:, :, :], oh1[:, :, :], oh2[:, :, :], ALU.add).then_inc(r_sel, 1)
                dve.wait_ge(r_sel, v)
                past(dve, f_cf, 2 * NK * b)
                dve.tensor_tensor(cfx[:, :, H:H + E], sel[:, :, :], gact[:, :, :], ALU.mult).then_inc(r_cf, 1)

            def gate(b, h):
                u = 2 * b + h
                past(dve, f_dn[h], b + FREE)
                for k in range(NK):
                    j = NK * u + k
                    src = bank[:, 4 + (NK * h + k) % 2, :]
                    dve.wait_ge(f_cf, j + 1)
                    if k < NB:
                        dve.wait_ge(f_silu, j + 1 + FREE)
                        dve.tensor_tensor(gt[:, h, k, :], hs[:, k, :], src, ALU.mult).then_inc(f_g, 1)
                    else:
                        dve.tensor_copy(gt[H:96, h, k, :], src[H:96, :]).then_inc(f_g, 1)

            def residual2(b, h):
                dve.wait_ge(f_dn[h], b + 1 + FREE)
                past(dve, stored[h], 16 * b + 16 * FREE)
                dve.tensor_tensor(yo[:, h, :, :].rearrange("p t q -> p (t q)"),
                                  ra[:, b, TH * h:TH * h + TH, :].rearrange("p t q -> p (t q)"),
                                  bank[:, 6, :], ALU.add).then_inc(f_out, 1)

            for h in range(2):
                norm1(0, h)
                residual1(0, h)
                norm2(0, h)
            dve.wait_ge(ld_rw, 32)
            dve.wait_ge(consts, 7 + E + 1)
            choose(0)
            with dve.Fori(0, B - 1) as b:
                for h in range(2):
                    norm1(b + 1, h)
                    gate(b, h)
                    residual1(b + 1, h)
                    norm2(b + 1, h)
                    residual2(b, h)
                choose(b + 1)
            for h in range(2):
                gate(B - 1, h)
                residual2(B - 1, h)


_INS = ['L0_attn_x', 'L0_attn_W_x', 'L0_attn_W_dt', 'L0_attn_b_dt', 'L0_attn_A_log', 'L0_attn_D',
        'L0_attn_W_out', 'L0_attn_b_out', 'L0_ffn_routing_W', 'L0_ffn_expert_bias', 'L0_ffn_sW1',
        'L0_ffn_sb1', 'L0_ffn_sW2', 'L0_ffn_sb2', 'L0_ffn_rW1', 'L0_ffn_rb1', 'L0_ffn_rW2', 'L0_ffn_rb2']


def kernel(**inputs):
    import numpy as np
    import concourse.bacc as bacc
    from concourse import mybir as mb
    from concourse.bass_utils import run_bass_kernel_spmd

    nc = bacc.Bacc("TRN2", target_bir_lowering=False, num_devices=1)
    arrays, args = {}, []
    for name in _INS:
        a = np.ascontiguousarray(inputs[name])
        arrays[f"in_{name}"] = a
        args.append(nc.dram_tensor(f"in_{name}", a.shape, mb.dt.from_np(a.dtype), kind="ExternalInput").ap())
    shape = arrays["in_L0_attn_x"].shape
    args.append(nc.dram_tensor("out", shape, mb.dt.float32, kind="ExternalOutput").ap())
    build(nc, *args)
    r = run_bass_kernel_spmd(nc, [arrays], core_ids=[0])
    return r.results[0]["out"]
```

```python
from contextlib import ExitStack

import concourse.bass as bass
from concourse import mybir

ALU = mybir.AluOpType
ACT = mybir.ActivationFunctionType
AX = mybir.AxisListType
F32 = mybir.dt.float32
I32 = mybir.dt.int32

P = 128
FREE = 1
LN_EPS = 1e-5
LOG_TINY = 27.631021115928547
UNDERFLOW = -104.0
TAKEN = -1e30
TINY = 1e-30
LEAST = 1e-18

CLASSES = [(0, 1, 256, 2), (1, 2, 128, 4), (3, 4, 64, 2), (7, 8, 32, 4), (15, 1, 32, 6)]
TAIL = 256


def build(nc, x, W_x, W_dt, b_dt, A_log, D, W_out, b_out, routing_W, expert_bias,
          sW1, sb1, sW2, sb2, rW1, rb1, rW2, rb2, out):
    B, L, DM = x.shape
    R = W_dt.shape[0]
    N = A_log.shape[1]
    E, _, H = rW1.shape
    T = L // P
    TT = TAIL // P
    TH = T // 2
    HT = TH * P
    TB = B * TT
    J = T // TT
    U = 2 * J
    UA = U - 2
    NB = E * H // P
    EB = P // H
    KX = H + E + 1
    SEG = TAIL + 1
    assert DM == P and H == 64 and N == 16 and L % HT == 0 and B == 4

    offs, total = [], 0
    for _, ns, w, _ in CLASSES:
        offs.append(total)
        total += ns * B * w

    ctx = ExitStack()
    with ctx:
        def sb(name, shape, dt=F32):
            return ctx.enter_context(nc.sbuf_tensor(name, shape, dt))

        def sem(name):
            return ctx.enter_context(nc.semaphore(name))

        bank = ctx.enter_context(nc.psum_tensor("bank", [P, 8, 512], F32))

        ident = sb("ident", [P, P])
        ramp = sb("ramp", [P, E])
        mask = sb("mask", [P, B * SEG])
        wx = sb("wx", [P, R + 2 * N])
        wxT = sb("wxT", [R, P])
        wdt = sb("wdt", [R, P])
        wcomb = sb("wcomb", [P, P])
        wout = sb("wout", [P, P])
        dwout = sb("dwout", [P, P])
        alog = sb("alog", [P, N])
        aneg = sb("aneg", [P, N])
        aval = sb("aval", [P, N])
        dcol = sb("dcol", [P, 1])
        bdt = sb("bdt", [P, 1])
        bout = sb("bout", [P, P])
        rw = sb("rw", [E, P])
        rwT = sb("rwT", [P, E])
        ebias = sb("ebias", [P, E])
        w1 = sb("w1", [P, (E + 1) * H])
        b1 = sb("b1", [P, NB + 1])
        w2 = sb("w2", [P, NB + 1, P])
        epsv = sb("epsv", [P, T])
        mhalf = sb("mhalf", [P, T])
        logt = sb("logt", [P, 1])

        xa = sb("xa", [P, J, B, TT, P])
        ra = sb("ra", [P, J, B, TT, P])

        tst = sb("tst", [P, TB, 6])
        tmv = sb("tmv", [P, TB, 2])
        trs = sb("trs", [P, TB])
        txn = sb("txn", [P, TB, P])
        txT = sb("txT", [P, TB, P])
        tab = sb("tab", [P, B, TAIL])
        tex = sb("tex", [P, B, TAIL])
        tre = sb("tre", [P, B, TAIL])
        tdl = sb("tdl", [P, B, SEG])
        tsu = sb("tsu", [P, B, SEG])
        tw = sb("tw", [P, B, TAIL])
        tbc = sb("tbc", [P, TB, 2 * N])
        gprod = sb("gprod", [P, N, B])
        gmax = sb("gmax", [P, 1])
        gmx1 = sb("gmx1", [1, 1])
        flag = sb("flag", [1, 1], I32)
        fa = sb("fa", [P, total])
        fs = sb("fs", [P, total])
        fv = sb("fv", [P, total])
        red = sb("red", [P, 3, B * P])
        yT = sb("yT", [P, B, TAIL])

        st1 = sb("st1", [P, 2, TH, 6])
        mv1 = sb("mv1", [P, 2, TH, 2])
        rs1 = sb("rs1", [P, 2, TH])
        xn1 = sb("xn1", [P, 2, TH, P])
        xT1 = sb("xT1", [P, 2, TH, P])
        st2 = sb("st2", [P, 2, TH, 6])
        mv2 = sb("mv2", [P, 2, TH, 2])
        rs2 = sb("rs2", [P, 2, TH])
        xn2 = sb("xn2", [P, 2, TH, P])
        xT2 = sb("xT2", [P, 2, HT])
        lg = sb("lg", [P, T, E])
        lga = sb("lga", [P, T, E])
        lge = sb("lge", [P, T, E])
        lsp = sb("lsp", [P, T, E])
        gact = sb("gact", [P, T, E])
        m1 = sb("m1", [P, T])
        p1 = sb("p1", [P, T])
        oh1 = sb("oh1", [P, T, E])
        oh2 = sb("oh2", [P, T, E])
        sel = sb("sel", [P, T, E])
        lgu = sb("lgu", [P, T, E])
        lgq = sb("lgq", [P, T, E])
        rest = sb("rest", [P, T, E])
        cfx = sb("cfx", [P, T, 96])
        hs = sb("hs", [P, NB, HT])
        gt = sb("gt", [P, 2, NB + 1, HT])
        yo = sb("yo", [P, 2, TH, P])

        def cut(t, at, n):
            return t[:, at:at + n]

        def tiles(v):
            return v.rearrange("p (t q) -> p t q", q=P)

        assert total >= 4 * L + 2
        gxn, gxT = tiles(cut(fa, 0, L)), tiles(cut(fa, L, L))
        gab, gre = cut(fa, 2 * L, L), cut(fa, 3 * L, L)
        gdl, gsu = cut(fs, 0, L + 1), cut(fs, L + 1, L + 1)
        gw, gd = cut(fs, 2 * L + 2, L), cut(fs, 3 * L + 2, L)
        gs, gv, gh, gy = cut(fv, 0, L), cut(fv, L, L), cut(fv, 2 * L, L), tiles(cut(fv, 3 * L, L))
        gst = sb("gst", [P, T, 6])
        gmv = sb("gmv", [P, T, 2])
        grs = sb("grs", [P, T])
        gbc = sb("gbc", [P, T, 2 * N])
        gbn = sb("gbn", [P, 2, T])
        gan = sb("gan", [P, 1])
        gtail = sb("gtail", [P, B, TAIL])

        wideg = cut(fs, 0, 2 * TH * E * H).rearrange("p (h t n) -> p h t n", h=2, t=TH)

        def sems(names):
            return [sem(n) for n in names.split()]

        ld_wx, ld_wout, ld_small, ld_bout, ld_ffn1, ld_ffn2, ld_rw = \
            sems("ld_wx ld_wout ld_small ld_bout ld_ffn1 ld_ffn2 ld_rw")
        ld_x = [sem(f"ld_x{j}") for j in range(J)]
        stored = sems("stored0 stored1")
        zeroed, consts, wxT_t, wxT_c, wcomb_p, wcomb_c, rwT_p, rwT_c, dwout_c, aneg_c, aval_c, res_init = \
            sems("zeroed consts wxT_t wxT_c wcomb_p wcomb_c rwT_p rwT_c dwout_c aneg_c aval_c res_init")
        t_st, t_mv, t_ve, t_rs, t_xn, t_tp, t_xT, t_z, t_ab, t_ex, t_re, t_ln, t_dl, t_su, t_w = \
            sems("t_st t_mv t_ve t_rs t_xn t_tp t_xT t_z t_ab t_ex t_re t_ln t_dl t_su t_w")
        t_bcp, t_bc, t_gp, t_gm, t_gt, t_g1, t_flag, t_B, t_C, t_v, t_a, t_a0, t_s, t_h, t_hs = \
            sems("t_bcp t_bc t_gp t_gm t_gt t_g1 t_flag t_B t_C t_v t_a t_a0 t_s t_h t_hs")
        t_zc, t_red, t_y, t_yall, t_o, t_res = sems("t_zc t_red t_y t_yall t_o t_res")
        g_st, g_mv, g_ve, g_rs, g_xn, g_tp, g_xT, g_z, g_bcp, g_bc, g_ab, g_ex, g_re, g_ln, g_dl = \
            sems("g_st g_mv g_ve g_rs g_xn g_tp g_xT g_z g_bcp g_bc g_ab g_ex g_re g_ln g_dl")
        g_zero, g_su, g_w, g_col, g_BC, g_a, g_s, g_v, g_h, g_hs, g_zc, g_y, g_o, g_res, g_yT = \
            sems("g_zero g_su g_w g_col g_BC g_a g_s g_v g_h g_hs g_zc g_y g_o g_res g_yT")
        s_st, s_mv, s_ve, s_rs, s_xn, s_xT, s_o, s_x1 = sems("s_st s_mv s_ve s_rs s_xn s_xT s_o s_x1")
        n_st, n_mv, n_ve, n_rs, n_xn, n_xT = sems("n_st n_mv n_ve n_rs n_xn n_xT")
        turned, turn_read = sems("turned turn_read")
        r_p, r_lg, r_ab, r_ex, r_ln, r_u, r_u1, r_rc, r_q, r_tq, r_spq, r_sp, r_lnsp, r_act = \
            sems("r_p r_lg r_ab r_ex r_ln r_u r_u1 r_rc r_q r_tq r_spq r_sp r_lnsp r_act")
        r_m1, r_eq1, r_w1, r_p1, r_oh1, r_rest, r_m2, r_eq2, r_w2, r_p2, r_oh2, r_sel, r_cf = \
            sems("r_m1 r_eq1 r_w1 r_p1 r_oh1 r_rest r_m2 r_eq2 r_w2 r_p2 r_oh2 r_sel r_cf")
        f_wide, f_up, f_silu, f_cf, f_g, f_gx, f_dn, f_out = \
            sems("f_wide f_up f_silu f_cf f_g f_gx f_dn f_out")
        waited = sem("waited")

        block = ctx.enter_context(nc.Block())

        x_v = x.rearrange("b (j s p) d -> p j b s d", j=J, p=P)
        out_v = out.rearrange("b (j s p) d -> p j b s d", j=J, p=P)
        GENERAL = 1
        NK = NB + 1

        def col(v):
            return v.rearrange("(p a) -> p a", a=1)

        def row_bc(v):
            return v.rearrange("(a n) -> a n", a=1).to_broadcast([P, v.shape[0]])

        def past(eng, semaphore, count):
            if not (isinstance(count, int) and count <= 0):
                eng.wait_ge(semaphore, count)

        def stop_for(eng, semaphore, count):
            eng.wait_ge(semaphore, count)
            eng.sem_inc(waited, 1)

        def unit(t, u):
            h = B // 2 * (u % 2)
            return t[:, u // 2, h:h + B // 2, :, :].rearrange("p b s d -> p (b s) d")

        def seq(v):
            return v.rearrange("p j s d -> p (j s) d")

        TURNS = [("first", 0), ("first", 1), ("second", 0), ("second", 1), ("first", 2), ("first", 3)]
        for u in range(U):
            TURNS += [("second", u + 2)] * (u + 2 < U) + [("first", u + 4)] * (u + 4 < UA)

        def flat(t, c):
            _, ns, w, _ = CLASSES[c]
            return t[:, offs[c]:offs[c] + ns * B * w]

        def wide(t, c):
            _, ns, w, _ = CLASSES[c]
            return flat(t, c).rearrange("p (n b w) -> p n b w", n=ns, b=B)

        banks = bank[:, :, :].rearrange("p k n -> p (k n)")

        def psum_class(c):
            _, ns, w, first = CLASSES[c]
            return banks[:, 512 * first:512 * first + ns * B * w]

        def two(k):
            return banks[:, 512 * k:512 * (k + 2)]

        @block.sync
        def _(sp):
            for j in (J - 1, *range(J - 1)):
                for b in range(B):
                    sp.dma_start(xa[:, j, b, :, :], x_v[:, j, b, :, :]).then_inc(ld_x[j], 16)
            for u in range(U):
                h = B // 2 * (u % 2)
                sp.wait_ge(f_out, u + 1)
                for b in range(B // 2):
                    sp.dma_start(out_v[:, u // 2, h + b, :, :], yo[:, u % 2, TT * b:TT * b + TT, :])\
                      .then_inc(stored[u % 2], 16)
            for h in range(2):
                sp.wait_ge(stored[h], 16 * B // 2 * J)

        @block.gpsimd
        def _(pool):
            pool.memset(ident[:, :], 0.0).then_inc(zeroed, 1)
            pool.wait_ge(zeroed, 1)
            pool.affine_select(out=ident[:, :], in_=ident[:, :], compare_op=ALU.not_equal, fill=1.0,
                               base=0, pattern=[[-1, P]], channel_multiplier=1).then_inc(consts, 1)
            pool.memset(epsv[:, :], LN_EPS).then_inc(consts, 1)
            pool.memset(mhalf[:, :], -0.5).then_inc(consts, 1)
            pool.memset(logt[:, :], LOG_TINY).then_inc(consts, 1)
            pool.memset(mask[:, :], 1.0).then_inc(zeroed, 1)
            pool.memset(tdl[:, :, TAIL:SEG], 0.0).then_inc(consts, 1)
            pool.wait_ge(zeroed, 2)
            pool.memset(mask[:, TAIL::SEG], 0.0).then_inc(consts, 1)
            for e in range(E):
                pool.memset(ramp[:, e:e + 1], float(E - e)).then_inc(consts, 1)
            pool.memset(cfx[:, :, :], 0.0).then_inc(zeroed, 1)
            pool.wait_ge(zeroed, 3)
            pool.memset(cfx[:, :, H + E:KX], 1.0).then_inc(consts, 1)

            def inv_sqrt(rs, mv, n, mv_ready, sum_ready, ready, u):
                pool.wait_ge(mv_ready, u + 1)
                pool.tensor_tensor(rs, mv, epsv[:, 0:n], ALU.add).then_inc(sum_ready, 1)
                pool.wait_ge(sum_ready, u + 1)
                pool.tensor_tensor(rs, rs, mhalf[:, 0:n], ALU.pow).then_inc(ready, 1)

            pool.wait_ge(consts, 3)
            inv_sqrt(trs[:, :], tmv[:, :, 1], TB, t_mv, t_ve, t_rs, 0)

            def norm1(u):
                inv_sqrt(rs1[:, u % 2, :], mv1[:, u % 2, :, 1], TH, s_mv, s_ve, s_rs, u)

            def norm2(u):
                inv_sqrt(rs2[:, u % 2, :], mv2[:, u % 2, :, 1], TH, n_mv, n_ve, n_rs, u)

            def with_bias(u):
                pool.wait_ge(ld_x[u // 2], 16 * B)
                pool.tensor_tensor(unit(ra, u), unit(xa, u),
                                   bout[:, :].unsqueeze(1).to_broadcast([P, TH, P]),
                                   ALU.add).then_inc(res_init, 1)

            norm1(0)
            norm1(1)
            pool.wait_ge(ld_bout, 16)
            with_bias(0)
            with_bias(1)
            pool.wait_ge(t_dl, 1)
            pool.wait_ge(t_xT, 2)
            pool.tensor_tensor(tw[:, :, :], tdl[:, :, 0:TAIL],
                               txT[:, :, :].rearrange("p (b s) q -> p b (s q)", b=B),
                               ALU.mult).then_inc(t_w, 1)
            for u in range(2, U):
                with_bias(u)

            pool.wait_ge(t_flag, 1)
            with pool.If(pool.value_load(flag[0:1, 0:1], min_val=0, max_val=1) == GENERAL):
                with pool.Fori(0, B) as b:
                    inv_sqrt(grs[:, :], gmv[:, :, 1], T, g_mv, g_ve, g_rs, b)
                pool.wait_ge(g_res, 2 * B)

            for c, (_, ns, w, _) in enumerate(CLASSES):
                pool.wait_ge(t_a, sum(q[1] for q in CLASSES[:c + 1]))
                pool.memset(flat(fa, c)[:, 0::w], 0.0).then_inc(t_a0, 1)
            norm2(0)
            norm2(1)
            for c in range(len(CLASSES)):
                pool.wait_ge(t_h, c + 1)
                pool.wait_ge(t_s, sum(q[1] for q in CLASSES[:c + 1]))
                pool.tensor_tensor(flat(fa, c), flat(fv, c), flat(fs, c), ALU.mult).then_inc(t_hs, 1)
            norm1(2)
            norm1(3)
            for u in range(U):
                if u + 2 < U:
                    norm2(u + 2)
                if u + 4 < UA:
                    norm1(u + 4)

        @block.scalar
        def _(act):
            act.dma_start(wx[:, :], W_x).then_inc(ld_wx, 16)
            act.dma_start(wdt[:, :], W_dt).then_inc(ld_wx, 16)
            act.dma_start(alog[:, :], A_log).then_inc(ld_small, 16)
            act.dma_start(bdt[:, :], col(b_dt)).then_inc(ld_small, 16)
            act.dma_start(dcol[:, :], col(D)).then_inc(ld_wout, 16)
            act.dma_start(wout[:, :], W_out).then_inc(ld_wout, 16)
            act.dma_start(bout[:, :], row_bc(b_out)).then_inc(ld_bout, 16)
            act.dma_start(rw[:, :], routing_W).then_inc(ld_rw, 16)
            act.dma_start(ebias[:, :], row_bc(expert_bias)).then_inc(ld_rw, 16)
            act.dma_start(w1[:, 0:E * H].rearrange("p (e h) -> p e h", e=E),
                          rW1.rearrange("e d h -> d e h")).then_inc(ld_ffn1, 16)
            act.dma_start(w1[:, E * H:(E + 1) * H], sW1).then_inc(ld_ffn1, 16)
            for k in range(NB):
                act.dma_start(b1[:, k:k + 1], rb1[EB * k:EB * k + EB, :].rearrange("e (h a) -> (e h) a", a=1))\
                   .then_inc(ld_ffn1, 16)
            act.dma_start(b1[0:H, NB:NK], col(sb1)).then_inc(ld_ffn1, 16)
            for k in range(NB):
                act.dma_start(w2[:, k, :], rW2[EB * k:EB * k + EB, :, :].rearrange("e h d -> (e h) d"))\
                   .then_inc(ld_ffn2, 16)
            act.dma_start(w2[0:H, NB, :], sW2).then_inc(ld_ffn2, 16)
            act.dma_start(w2[H:H + E, NB, :], rb2).then_inc(ld_ffn2, 16)
            act.dma_start(w2[H + E:KX, NB, :], sb2.rearrange("(a d) -> a d", a=1)).then_inc(ld_ffn2, 16)

            act.wait_ge(ld_small, 32)
            act.activation(aneg[:, :], alog[:, :], ACT.Exp).then_inc(aneg_c, 1)
            act.wait_ge(aneg_c, 1)
            act.mul(aval[:, :], aneg[:, :], -1.0).then_inc(aval_c, 1)
            act.wait_ge(wxT_t, 1)
            act.copy(wxT[:, :], bank[0:R, 7, 0:P]).then_inc(wxT_c, 1)
            act.wait_ge(rwT_p, 1)
            act.copy(rwT[:, :], bank[:, 1, 0:E]).then_inc(rwT_c, 1)
            act.wait_ge(wcomb_p, 1)
            act.copy(wcomb[:, :], bank[:, 2, 0:P]).then_inc(wcomb_c, 1)
            for k in range(2):
                act.wait_ge(t_tp, k + 1)
                act.copy(txT[:, TB // 2 * k:TB // 2 * (k + 1), :].rearrange("p t q -> p (t q)"),
                         bank[:, 5 + k, :]).then_inc(t_xT, 1)
            act.wait_ge(t_z, 1)
            act.activation(tre[:, :, :].rearrange("p b w -> p (b w)"), two(2), ACT.Relu,
                           bias=bdt[:, :]).then_inc(t_re, 1)
            act.activation(tab[:, :, :].rearrange("p b w -> p (b w)"), two(2), ACT.Abs,
                           bias=bdt[:, :]).then_inc(t_ab, 1)
            act.wait_ge(t_ab, 1)
            act.activation(tex[:, :, :], tab[:, :, :], ACT.Exp, scale=-1.0).then_inc(t_ex, 1)
            act.wait_ge(t_ex, 1)
            act.activation(tab[:, :, :], tex[:, :, :], ACT.Ln, bias=1.0).then_inc(t_ln, 1)
            act.wait_ge(t_bcp, 1)
            act.copy(tbc[:, :, :].rearrange("p t n -> p (t n)"), bank[:, 4, 0:TB * 2 * N]).then_inc(t_bc, 1)

            def turn_out(kind, u, dst):
                n = TURNS.index((kind, u))
                act.wait_ge(turned, n + 1)
                return act.copy(dst, bank[:, 0, :]).then_inc(turn_read, 1)

            def evac1(u):
                past(act, s_o, u - 1)
                turn_out("first", u, xT1[:, u % 2, :, :].rearrange("p t q -> p (t q)"))

            def evac2(u):
                past(act, f_up, NK * (u - 1))
                past(act, r_p, u - 1)
                turn_out("second", u, xT2[:, u % 2, :])

            evac1(0)
            evac1(1)

            act.wait_ge(t_flag, 1)
            with act.If(act.value_load(flag[0:1, 0:1], min_val=0, max_val=1) == GENERAL):
                with act.Fori(0, B) as b:
                    act.wait_ge(g_tp, b + 1)
                    act.copy(gxT[:, :, :].rearrange("p t q -> p (t q)"), two(0)).then_inc(g_xT, 1)
                    act.wait_ge(g_z, b + 1)
                    act.activation(gre[:, :], two(2), ACT.Relu, bias=bdt[:, :]).then_inc(g_re, 1)
                    act.activation(gab[:, :], two(2), ACT.Abs, bias=bdt[:, :]).then_inc(g_ab, 1)
                    act.wait_ge(g_ab, b + 1)
                    act.activation(gd[:, :], gab[:, :], ACT.Exp, scale=-1.0).then_inc(g_ex, 1)
                    act.wait_ge(g_ex, b + 1)
                    act.activation(gab[:, :], gd[:, :], ACT.Ln, bias=1.0).then_inc(g_ln, 1)
                    act.wait_ge(g_bcp, b + 1)
                    act.copy(gbc[:, :, :].rearrange("p t n -> p (t n)"), bank[:, 4, 0:T * 2 * N]).then_inc(g_bc, 1)
                    stop_for(act, g_su, b + 1)
                    with act.Fori(0, N) as n:
                        i = N * b + n
                        act.wait_ge(g_col, 3 * i + 3)
                        act.wait_ge(g_h, i + FREE)
                        act.activation(gd[:, :], gdl[:, 0:L], ACT.Exp, scale=gan[:, :]).then_inc(g_a, 1)
                        act.wait_ge(g_hs, i + FREE)
                        act.activation(gs[:, :], gsu[:, 1:L + 1], ACT.Sigmoid, scale=gan[:, :],
                                       bias=logt[:, :]).then_inc(g_s, 1)
                act.wait_ge(g_res, 2 * B)

            act.wait_ge(t_dl, 1)
            act.wait_ge(aval_c, 1)
            for c, (k0, ns, w, _) in enumerate(CLASSES):
                for n in range(ns):
                    act.activation(wide(fa, c)[:, n], tdl[:, :, TAIL - w:TAIL], ACT.Exp,
                                   scale=aval[:, k0 + n:k0 + n + 1]).then_inc(t_a, 1)
            act.wait_ge(t_su, 1)
            act.wait_ge(consts, 4)
            for c, (k0, ns, w, _) in enumerate(CLASSES):
                for n in range(ns):
                    act.activation(wide(fs, c)[:, n], tsu[:, :, SEG - w:SEG], ACT.Sigmoid,
                                   scale=aval[:, k0 + n:k0 + n + 1], bias=logt[:, :]).then_inc(t_s, 1)
            evac2(0)
            evac2(1)

            def gates(j):
                v = j + 1
                act.wait_ge(r_lg, v)
                act.activation(lga[:, :, :], lg[:, :, :], ACT.Abs).then_inc(r_ab, 1)
                act.wait_ge(r_ab, v)
                act.activation(lge[:, :, :], lga[:, :, :], ACT.Exp, scale=-1.0).then_inc(r_ex, 1)
                act.wait_ge(r_ex, v)
                act.activation(lga[:, :, :], lge[:, :, :], ACT.Ln, bias=1.0).then_inc(r_ln, 1)
                act.wait_ge(r_sp, v)
                act.activation(lga[:, :, :], lsp[:, :, :], ACT.Ln).then_inc(r_lnsp, 1)
                act.wait_ge(r_lnsp, v)
                act.activation(gact[:, :, :], lga[:, :, :], ACT.Exp, scale=0.5).then_inc(r_act, 1)

            def widen(u):
                act.wait_ge(r_cf, u // 2 + 1)
                past(act, f_cf, NK * (u - 1))
                t0 = TH * (u % 2)
                act.copy(wideg[:, u % 2, :, :].rearrange("p t (e h) -> p t e h", e=E),
                         cfx[:, t0:t0 + TH, H:H + E].unsqueeze(3).to_broadcast([P, TH, E, H]))\
                   .then_inc(f_wide, 1)

            def silu(u):
                past(act, f_g, NB * u)
                past(act, f_dn, u - 1)
                for k in range(NK):
                    act.wait_ge(f_up, NK * u + k + 1)
                    src = bank[:, 2 + (NK * u + k) % 2, :]
                    if k < NB:
                        act.activation(hs[:, k, :], src, ACT.Silu, bias=b1[:, k:k + 1]).then_inc(f_silu, 1)
                    else:
                        act.activation(gt[0:H, u % 2, k, :], src[0:H, :], ACT.Silu,
                                       bias=b1[0:H, k:k + 1]).then_inc(f_silu, 1)
                act.wait_ge(f_cf, NK * u + NK)
                act.copy(gt[H:96, u % 2, NB, :], bank[H:96, 4 + (NK * u + NB) % 2, :]).then_inc(f_gx, 1)

            act.wait_ge(ld_ffn1, 16 * (NB + 3))
            gates(0)
            evac1(2)
            evac1(3)
            for u in range(U):
                widen(u)
                silu(u)
                if u + 2 < U:
                    evac2(u + 2)
                if u % 2 and u + 1 < U:
                    gates(u // 2 + 1)
                if u + 4 < UA:
                    evac1(u + 4)

        @block.tensor
        def _(pe):
            pe.wait_ge(consts, 1)
            pe.wait_ge(ld_wx, 32)
            pe.transpose(bank[0:R, 7, 0:P], wx[:, 0:R], ident[:, :]).then_inc(wxT_t, 1)
            pe.wait_ge(ld_rw, 32)
            pe.transpose(bank[:, 1, 0:E], rw[:, :], ident[0:E, 0:E]).then_inc(rwT_p, 1)
            pe.wait_ge(wxT_c, 1)
            pe.matmul(bank[:, 2, 0:P], wxT[:, :], wdt[:, :], start=True, stop=True).then_inc(wcomb_p, 1)
            for k in range(2):
                for j in range(TB // 2):
                    q = TB // 2 * k + j
                    pe.wait_ge(t_xn, q + 1)
                    mm = pe.transpose(bank[:, 5 + k, P * j:P * j + P], txn[:, q, :], ident[:, :])
                mm.then_inc(t_tp, 1)
            pe.wait_ge(wcomb_c, 1)
            for k in range(2):
                pe.wait_ge(t_xT, k + 1)
                mm = pe.matmul(bank[:, 2 + k, :], wcomb[:, :],
                               txT[:, TB // 2 * k:TB // 2 * (k + 1), :].rearrange("p t q -> p (t q)"),
                               start=True, stop=True)
            mm.then_inc(t_z, 1)
            for q in range(TB):
                mm = pe.matmul(bank[:, 4, 2 * N * q:2 * N * (q + 1)], txT[:, q, :], wx[:, R:R + 2 * N],
                               start=True, stop=True)
            mm.then_inc(t_bcp, 1)

            def turn(kind, u, src, ready):
                pe.wait_ge(ready, u + 1)
                past(pe, turn_read, TURNS.index((kind, u)))
                for t in range(TH):
                    mm = pe.transpose(bank[:, 0, P * t:P * t + P], src[:, u % 2, t, :], ident[:, :])
                mm.then_inc(turned, 1)

            def turn1(u):
                turn("first", u, xn1, s_xn)

            def turn2(u):
                turn("second", u, xn2, n_xn)

            turn1(0)
            turn1(1)
            pe.wait_ge(t_gm, 1)
            pe.wait_ge(rwT_c, 1)
            pe.transpose(bank[0:1, 7, 0:P], gmax[:, :], ident[:, :]).then_inc(t_gt, 1)

            pe.wait_ge(t_flag, 1)
            with pe.If(pe.value_load(flag[0:1, 0:1], min_val=0, max_val=1) == GENERAL):
                pe.wait_ge(turn_read, 2)
                with pe.Fori(0, B) as b:
                    pe.wait_ge(g_xn, b + 1)
                    for t in range(T):
                        mm = pe.transpose(banks[:, P * t:P * t + P], gxn[:, t, :], ident[:, :])
                    mm.then_inc(g_tp, 1)
                    pe.wait_ge(g_xT, b + 1)
                    for k in range(2):
                        mm = pe.matmul(bank[:, 2 + k, :], wcomb[:, :],
                                       gxT[:, TH * k:TH * (k + 1), :].rearrange("p t q -> p (t q)"),
                                       start=True, stop=True)
                    mm.then_inc(g_z, 1)
                    for t in range(T):
                        mm = pe.matmul(bank[:, 4, 2 * N * t:2 * N * (t + 1)], gxT[:, t, :],
                                       wx[:, R:R + 2 * N], start=True, stop=True)
                    mm.then_inc(g_bcp, 1)
                    stop_for(pe, g_dl, b + 1)
                    with pe.Fori(0, N) as n:
                        i = N * b + n
                        pe.wait_ge(g_col, 3 * i + 3)
                        pe.wait_ge(g_zc, i + FREE)
                        for s in range(2):
                            for t in range(T):
                                mm = pe.transpose(banks[:, 1024 * (1 + s) + P * t:1024 * (1 + s) + P * t + P],
                                                  gbn[:, s, t:t + 1].to_broadcast([P, P]), ident[:, :])
                        mm.then_inc(g_BC, 1)
                    pe.wait_ge(g_y, N * b + N)
                    for t in range(T):
                        mm = pe.matmul(banks[:, 3072 + P * t:3072 + P * t + P], gy[:, t, :], wout[:, :],
                                       start=True, stop=True)
                    mm.then_inc(g_o, 1)
                pe.wait_ge(g_res, 2 * B)

            def spread(c, column):
                k0, ns, w, first = CLASSES[c]
                parts = max(1, w // P)
                rows = min(w, P)
                lo = P - rows
                for n in range(ns):
                    for b in range(B):
                        for s in range(parts):
                            at = 512 * first + (n * B + b) * w + s * P
                            src = tbc[lo:P, TT * b + TT - parts + s, column + k0 + n:column + k0 + n + 1]
                            mm = pe.transpose(banks[:, at:at + rows], src.to_broadcast([rows, P]),
                                              ident[lo:P, lo:P])
                return mm

            def attn_out(u):
                pe.wait_ge(turn_read, TURNS.index(("first", u)) + 1)
                past(pe, s_x1, u)
                for t in range(TH):
                    mm = pe.matmul(bank[:, 1, P * t:P * t + P], xT1[:, u % 2, t, :], dwout[:, :],
                                   start=True, stop=True)
                mm.then_inc(s_o, 1)

            def router(u):
                pe.wait_ge(turn_read, TURNS.index(("second", u)) + 1)
                past(pe, r_lg, u // 2)
                at = TH * E * (u % 2)
                for t in range(TH):
                    mm = pe.matmul(bank[:, 7, at + E * t:at + E * t + E], xT2[:, u % 2, P * t:P * t + P],
                                   rwT[:, :], start=True, stop=True)
                mm.then_inc(r_p, 1)

            def up(u, k):
                j = NK * u + k
                m = P if k < NB else H
                past(pe, f_silu, j - 1)
                pe.matmul(bank[0:m, 2 + j % 2, :], w1[:, P * k:P * k + m], xT2[:, u % 2, :],
                          start=True, stop=True).then_inc(f_up, 1)

            def gates_up(u, k):
                if k == 0:
                    pe.wait_ge(f_wide, u + 1)
                if k == 1:
                    past(pe, f_gx, u)
                else:
                    past(pe, f_g, NB * u + max(k - 1, 0))
                for t in range(TH):
                    dst = bank[:, 4 + (NK * u + k) % 2, P * t:P * t + P]
                    if k < NB:
                        mm = pe.transpose(dst, wideg[:, u % 2, t, P * k:P * k + P], ident[:, :])
                    else:
                        mm = pe.transpose(dst[0:96, :], cfx[:, TH * (u % 2) + t, :], ident[:, :])
                mm.then_inc(f_cf, 1)

            def down(u):
                pe.wait_ge(f_g, NB * (u + 1))
                pe.wait_ge(f_gx, u + 1)
                pe.wait_ge(f_silu, NK * (u + 1))
                past(pe, f_out, u)
                for t in range(TH):
                    for k in range(NK):
                        rows = P if k < NB else KX
                        mm = pe.matmul(bank[:, 6, P * t:P * t + P], gt[0:rows, u % 2, k, P * t:P * t + P],
                                       w2[0:rows, k, :], start=(k == 0), stop=(k == NK - 1))
                mm.then_inc(f_dn, 1)

            pe.wait_ge(t_bc, 1)
            for c in range(len(CLASSES)):
                if c in (2, 3):
                    pe.wait_ge(t_v, c - 1)
                spread(c, 0).then_inc(t_B, 1)
            pe.wait_ge(dwout_c, 1)
            attn_out(0)
            attn_out(1)
            for c in range(len(CLASSES)):
                if c < 2:
                    pe.wait_ge(t_v, c + 3)
                elif c < 4:
                    pe.wait_ge(t_zc, c - 1)
                else:
                    pe.wait_ge(t_v, c + 1)
                spread(c, N).then_inc(t_C, 1)
                if c == 1:
                    turn2(0)
                    turn2(1)
                    router(0)
                    router(1)
            turn1(2)
            turn1(3)
            pe.wait_ge(t_yall, 1)
            for q in range(TB):
                dst = banks[:, 1024 + P * q:1024 + P * q + P]
                pe.matmul(dst, txT[:, q, :], dwout[:, :], start=True, stop=False)
                mm = pe.matmul(dst, yT[:, q // TT, P * (q % TT):P * (q % TT) + P], wout[:, :],
                               start=False, stop=True)
            mm.then_inc(t_o, 1)
            pe.wait_ge(t_res, 1)
            pe.wait_ge(ld_ffn1, 16 * (NB + 3))
            pe.wait_ge(ld_ffn2, 16 * (NB + 3))
            for u in range(U):
                if u + 2 < UA:
                    attn_out(u + 2)
                up(u, 0)
                up(u, 1)
                for k in range(NK):
                    gates_up(u, k)
                    if k + 2 < NK:
                        up(u, k + 2)
                if u + 2 < U:
                    turn2(u + 2)
                    router(u + 2)
                down(u)
                if u + 4 < UA:
                    turn1(u + 4)

        @block.vector
        def _(dve):
            for used in (g_h, g_hs, g_zc):
                dve.sem_inc(used, FREE)
            dve.wait_ge(ld_x[J - 1], 16 * B)
            for b in range(B):
                for s in range(TT):
                    q = TT * b + s
                    dve.bn_stats(tst[:, q, :], xa[:, J - 1, b, s, :]).then_inc(t_st, 1)
            for q in range(TB):
                dve.wait_ge(t_st, q + 1)
                mv = dve.bn_aggr(tmv[:, q, :], tst[:, q, :])
            mv.then_inc(t_mv, 1)
            dve.wait_ge(ld_wout, 32)
            dve.tensor_scalar(dwout[:, :], wout[:, :], dcol[:, :], None, ALU.mult).then_inc(dwout_c, 1)
            dve.wait_ge(t_rs, 1)
            for q in range(TB):
                dve.tensor_scalar(txn[:, q, :], xa[:, J - 1, q // TT, q % TT, :], tmv[:, q, 0:1],
                                  trs[:, q:q + 1], ALU.subtract, ALU.mult).then_inc(t_xn, 1)
            def inverse_norm_inputs(u, src, st, mv, stats_done, ready):
                for t in range(TH):
                    q = dve.bn_stats(st[:, u % 2, t, :], unit(src, u)[:, t, :])
                q.then_inc(stats_done, 1)
                dve.wait_ge(stats_done, u + 1)
                for t in range(TH):
                    q = dve.bn_aggr(mv[:, u % 2, t, :], st[:, u % 2, t, :])
                q.then_inc(ready, 1)

            def scale(u, src, mv, rs, dst, root_ready, ready):
                dve.wait_ge(root_ready, u + 1)
                for t in range(TH):
                    q = dve.tensor_scalar(dst[:, u % 2, t, :], unit(src, u)[:, t, :], mv[:, u % 2, t, 0:1],
                                          rs[:, u % 2, t:t + 1], ALU.subtract, ALU.mult)
                q.then_inc(ready, 1)

            def stats1(u):
                dve.wait_ge(ld_x[u // 2], 16 * B)
                inverse_norm_inputs(u, xa, st1, mv1, s_st, s_mv)

            def scale1(u):
                if u >= 2:
                    dve.wait_ge(turned, TURNS.index(("first", u - 2)) + 1)
                scale(u, xa, mv1, rs1, xn1, s_rs, s_xn)

            def stats2(u):
                inverse_norm_inputs(u, ra, st2, mv2, n_st, n_mv)

            def scale2(u):
                if u >= 2:
                    dve.wait_ge(turned, TURNS.index(("second", u - 2)) + 1)
                scale(u, ra, mv2, rs2, xn2, n_rs, n_xn)

            stats1(0)
            stats1(1)
            scale1(0)
            scale1(1)
            dve.wait_ge(t_ln, 1)
            dve.wait_ge(t_re, 1)
            dve.tensor_tensor(tdl[:, :, 0:TAIL], tre[:, :, :], tab[:, :, :], ALU.add).then_inc(t_dl, 1)
            dve.wait_ge(consts, 6)
            dve.wait_ge(t_dl, 1)
            dve.tensor_tensor_scan(tsu[:, :, :].rearrange("p b w -> p (b w)")[:, ::-1], mask[:, ::-1],
                                   tdl[:, :, :].rearrange("p b w -> p (b w)")[:, ::-1], 0.0,
                                   ALU.mult, ALU.add).then_inc(t_su, 1)
            dve.wait_ge(t_su, 1)
            dve.wait_ge(aval_c, 1)
            for c, (k0, ns, w, _) in enumerate(CLASSES):
                gp = dve.tensor_tensor(gprod[:, k0:k0 + ns, :],
                                       aval[:, k0:k0 + ns].unsqueeze(2).to_broadcast([P, ns, B]),
                                       tsu[:, :, TAIL - w].unsqueeze(1).to_broadcast([P, ns, B]), ALU.mult)
            gp.then_inc(t_gp, 1)
            dve.wait_ge(t_gp, 1)
            dve.tensor_reduce(gmax[:, :], gprod[:, :, :].rearrange("p n b -> p (n b)"), AX.X, ALU.max)\
               .then_inc(t_gm, 1)
            dve.wait_ge(t_gt, 1)
            dve.tensor_reduce(gmx1[:, :], bank[0:1, 7, 0:P], AX.X, ALU.max).then_inc(t_g1, 1)
            dve.wait_ge(t_g1, 1)
            dve.tensor_scalar(flag[:, :], gmx1[:, :], UNDERFLOW, None, ALU.is_ge).then_inc(t_flag, 1)

            dve.wait_ge(t_flag, 1)
            with dve.If(dve.value_load(flag[0:1, 0:1], min_val=0, max_val=1) == GENERAL):
                for j in range(J):
                    dve.wait_ge(ld_x[j], 16 * B)
                dve.wait_ge(res_init, U)
                dve.memset(gdl[:, L:L + 1], 0.0).then_inc(g_zero, 1)
                with dve.Fori(0, B) as b:
                    for t in range(T):
                        dve.bn_stats(gst[:, t, :], xa[:, t // TT, b, t % TT, :]).then_inc(g_st, 1)
                    stop_for(dve, g_st, T * b + T)
                    for t in range(T):
                        mv = dve.bn_aggr(gmv[:, t, :], gst[:, t, :])
                    mv.then_inc(g_mv, 1)
                    dve.wait_ge(g_rs, b + 1)
                    for t in range(T):
                        xn = dve.tensor_scalar(gxn[:, t, :], xa[:, t // TT, b, t % TT, :], gmv[:, t, 0:1],
                                               grs[:, t:t + 1], ALU.subtract, ALU.mult)
                    xn.then_inc(g_xn, 1)
                    dve.wait_ge(g_ln, b + 1)
                    dve.wait_ge(g_re, b + 1)
                    dve.tensor_tensor(gdl[:, 0:L], gre[:, :], gab[:, :], ALU.add).then_inc(g_dl, 1)
                    dve.wait_ge(g_dl, b + 1)
                    dve.wait_ge(g_zero, b + 1)
                    dve.tensor_tensor_scan(gsu[:, ::-1], mask[:, 0:1].to_broadcast([P, L + 1]),
                                           gdl[:, ::-1], 0.0, ALU.mult, ALU.add).then_inc(g_su, 1)
                    dve.tensor_tensor(gw[:, :], gdl[:, 0:L], gxT[:, :, :].rearrange("p t q -> p (t q)"),
                                      ALU.mult).then_inc(g_w, 1)
                    dve.memset(gy[:, :, :], 0.0).then_inc(g_zero, 1)
                    dve.wait_ge(g_zero, b + 2)
                    dve.wait_ge(g_bc, b + 1)
                    stop_for(dve, g_w, b + 1)
                    with dve.Fori(0, N) as n:
                        i = N * b + n
                        dve.tensor_copy(gbn[:, 0, :], gbc[:, :, n]).then_inc(g_col, 1)
                        dve.tensor_copy(gbn[:, 1, :], gbc[:, :, N + n]).then_inc(g_col, 1)
                        dve.tensor_copy(gan[:, :], aval[:, bass.ds(n, 1)]).then_inc(g_col, 1)
                        dve.wait_ge(g_BC, i + 1)
                        dve.tensor_tensor(gv[:, :], gw[:, :], two(2), ALU.mult).then_inc(g_v, 1)
                        dve.wait_ge(g_v, i + 1)
                        dve.wait_ge(g_a, i + 1)
                        dve.tensor_tensor_scan(gh[:, :], gd[:, :], gv[:, :], 0.0, ALU.mult, ALU.add)\
                           .then_inc(g_h, 1)
                        dve.wait_ge(g_h, i + 1 + FREE)
                        dve.wait_ge(g_s, i + 1)
                        dve.tensor_tensor(gv[:, :], gh[:, :], gs[:, :], ALU.mult).then_inc(g_hs, 1)
                        dve.wait_ge(g_hs, i + 1 + FREE)
                        dve.tensor_tensor(gh[:, :], gv[:, :], two(4), ALU.mult).then_inc(g_zc, 1)
                        dve.wait_ge(g_zc, i + 1 + FREE)
                        dve.tensor_tensor(gy[:, :, :].rearrange("p t q -> p (t q)"),
                                          gy[:, :, :].rearrange("p t q -> p (t q)"), gh[:, :],
                                          ALU.add).then_inc(g_y, 1)
                        dve.wait_ge(g_y, i + 1)
                    dve.wait_ge(g_o, b + 1)
                    earlier = ra[:, 0:J - 1, b, :, :].rearrange("p j s d -> p j (s d)")
                    dve.tensor_tensor(earlier, earlier,
                                      banks[:, 3072:3072 + P * (T - TT)].rearrange("p (j n) -> p j n", j=J - 1),
                                      ALU.add).then_inc(g_res, 1)
                    dve.tensor_copy(gtail[:, b, :], gy[:, T - TT:T, :].rearrange("p t q -> p (t q)"))\
                       .then_inc(g_res, 1)
                    stop_for(dve, g_res, 2 * b + 2)

            def scan_inputs(c):
                _, ns, w, _ = CLASSES[c]
                dve.wait_ge(t_w, 1)
                dve.wait_ge(t_B, c + 1)
                dve.tensor_tensor(wide(fv, c), psum_class(c).rearrange("p (n b w) -> p n b w", n=ns, b=B),
                                  tw[:, :, TAIL - w:TAIL].unsqueeze(1).to_broadcast([P, ns, B, w]),
                                  ALU.mult).then_inc(t_v, 1)

            def scan(c):
                dve.wait_ge(t_v, c + 1)
                dve.wait_ge(t_a0, c + 1)
                dve.tensor_tensor_scan(flat(fv, c), flat(fa, c), flat(fv, c), 0.0, ALU.mult, ALU.add)\
                   .then_inc(t_h, 1)

            def times_C(c):
                dve.wait_ge(t_C, c + 1)
                dve.wait_ge(t_hs, c + 1)
                dve.tensor_tensor(flat(fv, c), flat(fa, c), psum_class(c), ALU.mult).then_inc(t_zc, 1)

            def residual1(u):
                dve.wait_ge(s_o, u + 1)
                dve.wait_ge(res_init, u + 1)
                r = unit(ra, u)
                dve.tensor_tensor(r, r, bank[:, 1, :].rearrange("p (t q) -> p t q", t=TH), ALU.add)\
                   .then_inc(s_x1, 1)
                dve.wait_ge(s_x1, u + 1)

            def over_experts(t):
                return t[:, :].unsqueeze(2).to_broadcast([P, T, E])

            def small(op, dst, a, b, ready, v):
                dve.tensor_tensor(dst[:, :, :], a, b, op).then_inc(ready, 1)
                dve.wait_ge(ready, v)

            def most(dst, src, ready, v):
                dve.tensor_reduce(dst[:, :], src[:, :, :], AX.X, ALU.max).then_inc(ready, 1)
                dve.wait_ge(ready, v)

            def choose(j):
                v = j + 1
                ramps = ramp[:, :].unsqueeze(1).to_broadcast([P, T, E])
                dve.wait_ge(r_p, 2 * v)
                small(ALU.add, lg, bank[:, 7, 0:T * E].rearrange("p (t e) -> p t e", e=E),
                      ebias[:, :].unsqueeze(1).to_broadcast([P, T, E]), r_lg, v)
                most(m1, lg, r_m1, v)
                small(ALU.is_equal, oh1, lg[:, :, :], over_experts(m1), r_eq1, v)
                small(ALU.mult, oh2, oh1[:, :, :], ramps, r_w1, v)
                most(p1, oh2, r_p1, v)
                small(ALU.is_equal, oh1, ramps, over_experts(p1), r_oh1, v)
                dve.wait_ge(r_ex, v)
                dve.tensor_scalar(lgu[:, :, :], lge[:, :, :], 1.0, -1.0, ALU.add, ALU.add).then_inc(r_u, 1)
                dve.scalar_tensor_tensor(out=rest[:, :, :], in0=oh1[:, :, :], scalar=TAKEN,
                                         in1=lg[:, :, :], op0=ALU.mult, op1=ALU.add).then_inc(r_rest, 1)
                dve.wait_ge(r_u, v)
                dve.tensor_scalar(lgu[:, :, :], lgu[:, :, :], TINY, None, ALU.max).then_inc(r_u1, 1)
                dve.wait_ge(r_rest, v)
                most(m1, rest, r_m2, v)
                dve.wait_ge(r_u1, v)
                dve.reciprocal(lgu[:, :, :], lgu[:, :, :]).then_inc(r_rc, 1)
                small(ALU.is_equal, oh2, rest[:, :, :], over_experts(m1), r_eq2, v)
                dve.wait_ge(r_rc, v)
                dve.wait_ge(r_ln, v)
                dve.scalar_tensor_tensor(out=lgq[:, :, :], in0=lga[:, :, :], scalar=TINY,
                                         in1=lgu[:, :, :], op0=ALU.add, op1=ALU.mult).then_inc(r_q, 1)
                small(ALU.mult, rest, oh2[:, :, :], ramps, r_w2, v)
                dve.wait_ge(r_q, v)
                small(ALU.mult, lgu, lgq[:, :, :], lge[:, :, :], r_tq, v)
                dve.scalar_tensor_tensor(out=lgq[:, :, :], in0=lg[:, :, :], scalar=0.0, in1=lgu[:, :, :],
                                         op0=ALU.max, op1=ALU.add).then_inc(r_spq, 1)
                dve.wait_ge(r_spq, v)
                dve.tensor_scalar(lsp[:, :, :], lgq[:, :, :], LEAST, None, ALU.max).then_inc(r_sp, 1)
                most(p1, rest, r_p2, v)
                small(ALU.is_equal, oh2, ramps, over_experts(p1), r_oh2, v)
                small(ALU.add, sel, oh1[:, :, :], oh2[:, :, :], r_sel, v)
                past(dve, f_cf, 2 * NK * j)
                dve.wait_ge(r_act, v)
                dve.tensor_tensor(cfx[:, :, H:H + E], sel[:, :, :], gact[:, :, :], ALU.mult).then_inc(r_cf, 1)

            def gate(u):
                past(dve, f_dn, u - 1)
                for k in range(NB):
                    j = NK * u + k
                    dve.wait_ge(f_cf, j + 1)
                    dve.wait_ge(f_silu, j + 1)
                    dve.tensor_tensor(gt[:, u % 2, k, :], hs[:, k, :], bank[:, 4 + j % 2, :], ALU.mult)\
                       .then_inc(f_g, 1)

            def residual2(u):
                dve.wait_ge(f_dn, u + 1)
                past(dve, stored[u % 2], 16 * B // 2 * (u // 2))
                dve.tensor_tensor(yo[:, u % 2, :, :], unit(ra, u),
                                  bank[:, 6, :].rearrange("p (t q) -> p t q", t=TH), ALU.add)\
                   .then_inc(f_out, 1)

            for c in range(len(CLASSES)):
                scan_inputs(c)
            residual1(0)
            stats2(0)
            residual1(1)
            stats2(1)
            scan(0)
            scale2(0)
            scale2(1)
            for c in range(1, len(CLASSES)):
                scan(c)
            times_C(0)
            times_C(1)
            dve.wait_ge(ld_rw, 32)
            dve.wait_ge(consts, 6 + E + 1)
            choose(0)
            stats1(2)
            stats1(3)
            for c in range(2, len(CLASSES)):
                times_C(c)
            scale1(2)
            scale1(3)
            dve.wait_ge(t_zc, len(CLASSES))
            for i, c in enumerate((1, 2, 3)):
                _, ns, w, _ = CLASSES[c]
                dve.tensor_reduce(red[:, i, 0:B * w], wide(fv, c).rearrange("p n b w -> p (b w) n"),
                                  AX.X, ALU.add).then_inc(t_red, 1)
            dve.tensor_copy(yT[:, :, :], wide(fv, 0)[:, 0]).then_inc(t_y, 1)
            parts = [(red[:, i, 0:B * CLASSES[c][2]].rearrange("p (b w) -> p b w", b=B), CLASSES[c][2])
                     for i, c in enumerate((1, 2, 3))] + [(wide(fv, 4)[:, 0], CLASSES[4][2])]
            dve.wait_ge(t_red, 3)
            for i, (part, w) in enumerate(parts):
                dve.wait_ge(t_y, i + 1)
                dve.tensor_tensor(yT[:, :, TAIL - w:TAIL], yT[:, :, TAIL - w:TAIL], part, ALU.add)\
                   .then_inc(t_y, 1)
            dve.wait_ge(t_y, len(parts) + 1)
            with dve.If(dve.value_load(flag[0:1, 0:1], min_val=0, max_val=1) == GENERAL):
                dve.tensor_copy(yT[:, :, :], gtail[:, :, :]).then_inc(g_yT, 1)
                dve.wait_ge(g_yT, 1)
                dve.sem_inc(waited, 1)
            dve.sem_inc(t_yall, 1)
            dve.wait_ge(t_o, 1)
            dve.wait_ge(res_init, U)
            r = ra[:, J - 1, :, :, :].rearrange("p b s d -> p (b s d)")
            dve.tensor_tensor(r, r, two(2), ALU.add).then_inc(t_res, 1)
            dve.wait_ge(t_res, 1)

            for u in range(U):
                if u + 2 < UA:
                    residual1(u + 2)
                if u + 2 < U:
                    stats2(u + 2)
                    scale2(u + 2)
                if u >= 1:
                    residual2(u - 1)
                gate(u)
                if u % 2 and u + 1 < U:
                    choose(u // 2 + 1)
                if u + 4 < UA:
                    stats1(u + 4)
                    scale1(u + 4)
            residual2(U - 1)


_INS = ['L0_attn_x', 'L0_attn_W_x', 'L0_attn_W_dt', 'L0_attn_b_dt', 'L0_attn_A_log', 'L0_attn_D',
        'L0_attn_W_out', 'L0_attn_b_out', 'L0_ffn_routing_W', 'L0_ffn_expert_bias', 'L0_ffn_sW1',
        'L0_ffn_sb1', 'L0_ffn_sW2', 'L0_ffn_sb2', 'L0_ffn_rW1', 'L0_ffn_rb1', 'L0_ffn_rW2', 'L0_ffn_rb2']


def kernel(**inputs):
    import numpy as np
    import concourse.bacc as bacc
    from concourse import mybir as mb
    from concourse.bass_utils import run_bass_kernel_spmd

    nc = bacc.Bacc("TRN2", target_bir_lowering=False, num_devices=1)
    arrays, args = {}, []
    for name in _INS:
        a = np.ascontiguousarray(inputs[name])
        arrays[f"in_{name}"] = a
        args.append(nc.dram_tensor(f"in_{name}", a.shape, mb.dt.from_np(a.dtype), kind="ExternalInput").ap())
    shape = arrays["in_L0_attn_x"].shape
    args.append(nc.dram_tensor("out", shape, mb.dt.float32, kind="ExternalOutput").ap())
    build(nc, *args)
    r = run_bass_kernel_spmd(nc, [arrays], core_ids=[0])
    return r.results[0]["out"]
```

```python
from contextlib import ExitStack

import concourse.bass as bass
from concourse import mybir

ALU = mybir.AluOpType
ACT = mybir.ActivationFunctionType
AX = mybir.AxisListType
F32 = mybir.dt.float32
I32 = mybir.dt.int32
BF16 = mybir.dt.bfloat16

P = 128
FREE = 1
LN_EPS = 1e-5
LOG_TINY = 27.631021115928547
UNDERFLOW = -104.0
TAKEN = -1e30
TINY = 1e-30
LEAST = 1e-18

CLASSES = [(0, 1, 256, 2), (1, 2, 128, 4), (15, 1, 32, 6), (3, 4, 64, 2), (7, 8, 32, 4)]
SCANS = (0, 3, 1, 2, 4)
TAIL = 256
ROWS = 512
MANY_DECAYS, MANY_WEIGHTS = (4,), (3, 4)


def build(nc, x, W_x, W_dt, b_dt, A_log, D, W_out, b_out, routing_W, expert_bias,
          sW1, sb1, sW2, sb2, rW1, rb1, rW2, rb2, out):
    B, L, DM = x.shape
    R = W_dt.shape[0]
    N = A_log.shape[1]
    E, _, H = rW1.shape
    T = L // P
    TT = TAIL // P
    TH = T // 2
    HT = TH * P
    TB = B * TT
    J = T // TT
    U = 2 * J
    UA = U - 2
    NB = E * H // P
    NK = NB + 1
    EB = P // H
    GR = 3 * E + 1
    KX = H + GR
    SEG = TAIL + 1
    assert DM == P and H == 64 and N == 16 and L % HT == 0 and B == 4

    offs, total = [], 0
    for _, ns, w, _ in CLASSES:
        offs.append(total)
        total += ns * B * w
    CHUNKS = [(c, i) for c, (_, ns, w, _) in enumerate(CLASSES) for i in range(-(-ns * B * w // ROWS))]
    assert len(CHUNKS) == 9 and U == 8

    ctx = ExitStack()
    with ctx:
        def sb(name, shape, dt=F32):
            return ctx.enter_context(nc.sbuf_tensor(name, shape, dt))

        def sem(name):
            return ctx.enter_context(nc.semaphore(name))

        bank = ctx.enter_context(nc.psum_tensor("bank", [P, 8, 512], F32))

        ident = sb("ident", [P, P])
        identb = sb("identb", [P, P], BF16)
        average = sb("average", [P, P])
        pick = sb("pick", [GR, E, H], BF16)
        ramp = sb("ramp", [P, E])
        mask = sb("mask", [P, B * SEG])
        wx = sb("wx", [P, R + 2 * N])
        wxT = sb("wxT", [R, P])
        wdt = sb("wdt", [R, P])
        wcomb = sb("wcomb", [P, P])
        wout = sb("wout", [P, P])
        dwout = sb("dwout", [P, P])
        cwout = sb("cwout", [P, P])
        alog = sb("alog", [P, N])
        aneg = sb("aneg", [P, N])
        aval = sb("aval", [P, N])
        dcol = sb("dcol", [P, 1])
        bdt = sb("bdt", [P, 1])
        bout = sb("bout", [P, P])
        rw = sb("rw", [E, P])
        rwT = sb("rwT", [P, E])
        ebias = sb("ebias", [P, E])
        w1 = sb("w1", [P, (E + 1) * H])
        b1 = sb("b1", [P, NB + 1])
        w2 = sb("w2", [P, NB + 1, P])
        epsv = sb("epsv", [P, T])
        mhalf = sb("mhalf", [P, T])
        logt = sb("logt", [P, 1])

        xa = sb("xa", [P, J, B, TT, P])
        ra = sb("ra", [P, J, B, TT, P])

        tst = sb("tst", [P, TB, 6])
        tmv = sb("tmv", [P, TB, 2])
        trs = sb("trs", [P, TB])
        txn = sb("txn", [P, TB, P])
        txT = sb("txT", [P, TB, P])
        tab = sb("tab", [P, B, TAIL])
        tex = sb("tex", [P, B, TAIL])
        tre = sb("tre", [P, B, TAIL])
        tdl = sb("tdl", [P, B, SEG])
        tsu = sb("tsu", [P, B, SEG])
        tw = sb("tw", [P, B, TAIL])
        tbc = sb("tbc", [P, TB, 2 * N])
        gprod = sb("gprod", [P, N, B])
        gmax = sb("gmax", [P, 1])
        gmx1 = sb("gmx1", [1, 1])
        flag = sb("flag", [1, 1], I32)
        fa = sb("fa", [P, total])
        fs = sb("fs", [P, total])
        cs = sb("cs", [P, 2, ROWS])
        fv = sb("fv", [P, total])

        st1 = sb("st1", [P, UA, TH, 6])
        mv1 = sb("mv1", [P, UA, TH, 2])
        rs1 = sb("rs1", [P, UA, TH])
        xT1 = sb("xT1", [P, 2, TH, P])
        st2 = sb("st2", [P, 2, TH, 6])
        mv2 = sb("mv2", [P, 2, TH, 2])
        rs2 = sb("rs2", [P, 2, TH])
        xn2 = sb("xn2", [P, 2, TH, P])
        xT2 = sb("xT2", [P, 4, HT])
        lg = sb("lg", [P, T, E])
        lga = sb("lga", [P, T, E])
        lge = sb("lge", [P, T, E])
        lsp = sb("lsp", [P, T, E])
        gact = sb("gact", [P, T, E])
        m1 = sb("m1", [P, T])
        p1 = sb("p1", [P, T])
        oh1 = sb("oh1", [P, T, E])
        oh2 = sb("oh2", [P, T, E])
        gval = sb("gval", [P, T, E])
        grest = sb("grest", [P, T, E])
        lgu = sb("lgu", [P, T, E])
        lgq = sb("lgq", [P, T, E])
        lgr = sb("lgr", [P, T, E])
        rest = sb("rest", [P, T, E])
        g3 = sb("g3", [P, 2, T, GR], BF16)
        gT = sb("gT", [GR, 2, HT], BF16)
        hs = sb("hs", [P, NB, HT])
        gt = sb("gt", [P, 2, NB + 1, HT])
        yo = sb("yo", [P, 2, TH, P])

        def cut(t, at, n):
            return t[:, at:at + n]

        def tiles(v):
            return v.rearrange("p (t q) -> p t q", q=P)

        hs_flat = hs[:, :, :].rearrange("p k n -> p (k n)")
        xT2_flat = xT2[:, :, :].rearrange("p u n -> p (u n)")
        gt_flat = gt[:, :, :, :].rearrange("p u k n -> p (u k n)")
        assert L == 2 * HT and NB >= 4 and 2 * NK * HT >= 4 * L + 2 and total >= 4 * L
        gxn, gxT = tiles(cut(hs_flat, 0, L)), tiles(cut(hs_flat, L, L))
        gab, gre = cut(xT2_flat, 0, L), cut(xT2_flat, L, L)
        gdl, gsu = cut(gt_flat, 0, L + 1), cut(gt_flat, L + 1, L + 1)
        gw, gd = cut(gt_flat, 2 * L + 2, L), cut(gt_flat, 3 * L + 2, L)
        gs, gv, gh, gy = cut(fv, 0, L), cut(fv, L, L), cut(fv, 2 * L, L), tiles(cut(fv, 3 * L, L))
        gst = sb("gst", [P, T, 6])
        gmv = sb("gmv", [P, T, 2])
        grs = sb("grs", [P, T])
        gbc = sb("gbc", [P, T, 2 * N])
        gbn = sb("gbn", [P, 2, T])
        gan = sb("gan", [P, 1])
        gtail = sb("gtail", [P, B, TAIL])

        def sems(names):
            return [sem(n) for n in names.split()]

        ld_wx, ld_wout, ld_small, ld_bout, ld_ffn1, ld_ffn2, ld_rw = \
            sems("ld_wx ld_wout ld_small ld_bout ld_ffn1 ld_ffn2 ld_rw")
        ld_x = [sem(f"ld_x{j}") for j in range(J - 1)]
        ld_tail = sems("ld_tail0 ld_tail1")
        stored = sems("stored0 stored1")
        zeroed, consts, consts2, picked = sems("zeroed consts consts2 picked")
        wxT_t, wxT_c, wcomb_p, wcomb_c, rwT_p, rwT_c, dwout_c, avg_p, cwout_c = \
            sems("wxT_t wxT_c wcomb_p wcomb_c rwT_p rwT_c dwout_c avg_p cwout_c")
        aneg_c, aval_c, res_init = sems("aneg_c aval_c res_init")
        t_st, t_mv, t_ve, t_rs, t_xn, t_tp, t_xT, t_z, t_ab, t_ex, t_re, t_ln, t_dl, t_su, t_w = \
            sems("t_st t_mv t_ve t_rs t_xn t_tp t_xT t_z t_ab t_ex t_re t_ln t_dl t_su t_w")
        t_bcp, t_bc, t_gp, t_gm, t_gt, t_g1, t_flag, t_B, t_C, t_v, t_pa, t_ps, t_a, t_a0, t_s, t_h, t_cs, t_cw = \
            sems("t_bcp t_bc t_gp t_gm t_gt t_g1 t_flag t_B t_C t_v t_pa t_ps t_a t_a0 t_s t_h t_cs t_cw")
        t_zc, t_zd, t_sum, t_yall, t_own = sems("t_zc t_zd t_sum t_yall t_own")
        g_st, g_mv, g_ve, g_rs, g_xn, g_tp, g_xT, g_z, g_bcp, g_bc, g_ab, g_ex, g_re, g_ln, g_dl = \
            sems("g_st g_mv g_ve g_rs g_xn g_tp g_xT g_z g_bcp g_bc g_ab g_ex g_re g_ln g_dl")
        g_zero, g_su, g_w, g_col, g_BC, g_a, g_s, g_v, g_h, g_hs, g_zc, g_y, g_o, g_res, g_yT = \
            sems("g_zero g_su g_w g_col g_BC g_a g_s g_v g_h g_hs g_zc g_y g_o g_res g_yT")
        s_st, s_mv, s_ve, s_rs, s_o, s_x1 = sems("s_st s_mv s_ve s_rs s_o s_x1")
        n_st, n_mv, n_ve, n_rs, n_xn = sems("n_st n_mv n_ve n_rs n_xn")
        turned, turn_read = sems("turned turn_read")
        r_p, r_lg, r_ab, r_ex, r_ln, r_pos, r_u, r_u1, r_rc, r_l1, r_q, r_tq, r_spq, r_sp, r_lnsp, r_act = \
            sems("r_p r_lg r_ab r_ex r_ln r_pos r_u r_u1 r_rc r_l1 r_q r_tq r_spq r_sp r_lnsp r_act")
        r_m1, r_eq1, r_w1, r_p1, r_oh1, r_rest, r_m2, r_eq2, r_w2, r_p2, r_oh2, r_sel = \
            sems("r_m1 r_eq1 r_w1 r_p1 r_oh1 r_rest r_m2 r_eq2 r_w2 r_p2 r_oh2 r_sel")
        r_val, r_hi, r_rem, r_mid, r_cf = sems("r_val r_hi r_rem r_mid r_cf")
        f_up, f_silu, f_gT, f_cf, f_g, f_dn, f_out = sems("f_up f_silu f_gT f_cf f_g f_dn f_out")
        waited = sem("waited")

        block = ctx.enter_context(nc.Block())

        x_v = x.rearrange("b (j s p) d -> p j b s d", j=J, p=P)
        out_v = out.rearrange("b (j s p) d -> p j b s d", j=J, p=P)
        GENERAL = 1

        def col(v):
            return v.rearrange("(p a) -> p a", a=1)

        def row_bc(v):
            return v.rearrange("(a n) -> a n", a=1).to_broadcast([P, v.shape[0]])

        def past(eng, semaphore, count):
            if not (isinstance(count, int) and count <= 0):
                eng.wait_ge(semaphore, count)

        def stop_for(eng, semaphore, count):
            eng.wait_ge(semaphore, count)
            eng.sem_inc(waited, 1)

        def down_bank(u, t):
            return 1 if u == U - 1 and t >= TH // 2 else 6

        def unit(t, u):
            h = B // 2 * (u % 2)
            return t[:, u // 2, h:h + B // 2, :, :].rearrange("p b s d -> p (b s) d")

        TURNS = [("first", 0), ("first", 1), ("first", 2), ("first", 3), ("second", 0), ("second", 1),
                 ("first", 4), ("first", 5), ("gates", 0)]
        for u in range(1, U):
            if u % 2 and u + 1 < U:
                TURNS += [("second", u + 1), ("second", u + 2)]
            TURNS += [("gates", u)]

        def out_bank(u):
            return 6 if u == 1 else 1

        def turn_no(kind, u):
            return TURNS.index((kind, u)) + 1

        def flat(t, c):
            _, ns, w, _ = CLASSES[c]
            return t[:, offs[c]:offs[c] + ns * B * w]

        def wide(t, c):
            _, ns, w, _ = CLASSES[c]
            return flat(t, c).rearrange("p (n b w) -> p n b w", n=ns, b=B)

        def chunk(t, c, i):
            v = flat(t, c)
            return v[:, ROWS * i:min(ROWS * (i + 1), v.shape[1])]

        yT = wide(fv, 0)[:, 0]

        banks = bank[:, :, :].rearrange("p k n -> p (k n)")

        def psum_class(c):
            _, ns, w, first = CLASSES[c]
            return banks[:, 512 * first:512 * first + ns * B * w]

        def two(k):
            return banks[:, 512 * k:512 * (k + 2)]

        @block.sync
        def _(sp):
            def load_part(j):
                for b in range(B):
                    loaded = ld_x[j] if j < J - 1 else ld_tail[2 * b // B]
                    sp.dma_start(xa[:, j, b, :, :], x_v[:, j, b, :, :]).then_inc(loaded, 16)

            load_part(J - 1)
            load_part(0)
            sp.dma_start(bout[:, :], row_bc(b_out)).then_inc(ld_bout, 16)
            for j in range(1, J - 1):
                load_part(j)
            sp.dma_start(rw[:, :], routing_W).then_inc(ld_rw, 16)
            sp.dma_start(ebias[:, :], row_bc(expert_bias)).then_inc(ld_rw, 16)
            sp.dma_start(w1[:, 0:E * H].rearrange("p (e h) -> p e h", e=E),
                         rW1.rearrange("e d h -> d e h")).then_inc(ld_ffn1, 16)
            sp.dma_start(w1[:, E * H:(E + 1) * H], sW1).then_inc(ld_ffn1, 16)
            for k in range(NB):
                sp.dma_start(b1[:, k:k + 1], rb1[EB * k:EB * k + EB, :].rearrange("e (h a) -> (e h) a", a=1))\
                  .then_inc(ld_ffn1, 16)
            sp.dma_start(b1[0:H, NB:NK], col(sb1)).then_inc(ld_ffn1, 16)
            for k in range(NB):
                sp.dma_start(w2[:, k, :], rW2[EB * k:EB * k + EB, :, :].rearrange("e h d -> (e h) d"))\
                  .then_inc(ld_ffn2, 16)
            sp.dma_start(w2[0:H, NB, :], sW2).then_inc(ld_ffn2, 16)
            for i in range(3):
                sp.dma_start(w2[H + E * i:H + E * (i + 1), NB, :], rb2).then_inc(ld_ffn2, 16)
            sp.dma_start(w2[KX - 1:KX, NB, :], sb2.rearrange("(a d) -> a d", a=1)).then_inc(ld_ffn2, 16)
            for u in range(U):
                h = B // 2 * (u % 2)
                sp.wait_ge(f_out, u + 1)
                for b in range(B // 2):
                    if u == U - 1:
                        sp.wait_ge(f_out, U + b)
                    sp.dma_start(out_v[:, u // 2, h + b, :, :], yo[:, u % 2, TT * b:TT * b + TT, :])\
                      .then_inc(stored[u % 2], 16)
            for h in range(2):
                sp.wait_ge(stored[h], 16 * B // 2 * J)

        @block.gpsimd
        def _(pool):
            pool.memset(ident[:, :], 0.0).then_inc(zeroed, 1)
            pool.wait_ge(zeroed, 1)
            pool.affine_select(out=ident[:, :], in_=ident[:, :], compare_op=ALU.not_equal, fill=1.0,
                               base=0, pattern=[[-1, P]], channel_multiplier=1).then_inc(consts, 1)
            pool.memset(average[:, :], 1.0 / P).then_inc(consts, 1)
            pool.memset(epsv[:, :], LN_EPS).then_inc(consts, 1)
            pool.memset(mhalf[:, :], -0.5).then_inc(consts, 1)
            pool.memset(logt[:, :], LOG_TINY).then_inc(consts, 1)
            pool.memset(mask[:, :], 1.0).then_inc(zeroed, 1)
            pool.memset(tdl[:, :, TAIL:SEG], 0.0).then_inc(consts, 1)
            pool.wait_ge(zeroed, 2)
            pool.memset(mask[:, TAIL::SEG], 0.0).then_inc(consts, 1)

            def inv_sqrt(rs, mv, n, mv_ready, sum_ready, ready, u):
                pool.wait_ge(mv_ready, u + 1)
                pool.tensor_tensor(rs, mv, epsv[:, 0:n], ALU.add).then_inc(sum_ready, 1)
                pool.wait_ge(sum_ready, u + 1)
                pool.tensor_tensor(rs, rs, mhalf[:, 0:n], ALU.pow).then_inc(ready, 1)

            pool.memset(identb[:, :], 0.0).then_inc(zeroed, 1)
            pool.memset(pick[:, :, :], 0.0).then_inc(zeroed, 1)
            pool.memset(g3[:, :, :, GR - 1:GR], 1.0).then_inc(consts2, 1)
            for e in range(E):
                pool.memset(ramp[:, e:e + 1], float(E - e)).then_inc(consts2, 1)
            pool.wait_ge(zeroed, 4)
            pool.affine_select(out=identb[:, :], in_=identb[:, :], compare_op=ALU.not_equal, fill=1.0,
                               base=0, pattern=[[-1, P]], channel_multiplier=1).then_inc(consts2, 1)
            for i in range(3):
                if i:
                    pool.wait_ge(picked, i)
                pool.affine_select(out=pick[:, :, :], in_=pick[:, :, :], compare_op=ALU.not_equal, fill=1.0,
                                   base=-E * i, pattern=[[-1, E], [0, H]], channel_multiplier=1)\
                    .then_inc(picked, 1)

            pool.wait_ge(consts, 4)
            for k in range(2):
                tiles_k = slice(TB // 2 * k, TB // 2 * (k + 1))
                inv_sqrt(trs[:, tiles_k], tmv[:, tiles_k, 1], TB // 2, t_mv, t_ve, t_rs, k)

            def norm1(u):
                inv_sqrt(rs1[:, u, :], mv1[:, u, :, 1], TH, s_mv, s_ve, s_rs, u)

            def norm2(u):
                inv_sqrt(rs2[:, u % 2, :], mv2[:, u % 2, :, 1], TH, n_mv, n_ve, n_rs, u)

            def with_bias(u):
                if u < UA:
                    pool.wait_ge(ld_x[u // 2], 16 * B)
                else:
                    pool.wait_ge(ld_tail[u % 2], 16 * B // 2)
                pool.tensor_tensor(unit(ra, u), unit(xa, u),
                                   bout[:, :].unsqueeze(1).to_broadcast([P, TH, P]),
                                   ALU.add).then_inc(res_init, 1)

            pool.wait_ge(ld_bout, 16)
            with_bias(0)
            with_bias(1)
            norm1(0)
            norm1(1)
            with_bias(2)
            with_bias(3)
            with_bias(4)
            norm1(2)
            with_bias(5)

            def times_A(dst, src, c, ready):
                k0, ns, w, _ = CLASSES[c]
                pool.tensor_tensor(wide(dst, c), src.unsqueeze(1).to_broadcast([P, ns, B, w]),
                                   aval[:, k0:k0 + ns].unsqueeze(2).unsqueeze(3).to_broadcast([P, ns, B, w]),
                                   ALU.mult).then_inc(ready, 1)

            pool.wait_ge(t_dl, 2)
            pool.wait_ge(aval_c, 1)
            for c in MANY_DECAYS:
                times_A(fa, tdl[:, :, TAIL - CLASSES[c][2]:TAIL], c, t_pa)
            pool.wait_ge(t_xT, 2)
            pool.tensor_tensor(tw[:, :, :], tdl[:, :, 0:TAIL],
                               txT[:, :, :].rearrange("p (b s) q -> p b (s q)", b=B),
                               ALU.mult).then_inc(t_w, 1)

            pool.wait_ge(t_flag, 1)
            with pool.If(pool.value_load(flag[0:1, 0:1], min_val=0, max_val=1) == GENERAL):
                with pool.Fori(0, B) as b:
                    inv_sqrt(grs[:, :], gmv[:, :, 1], T, g_mv, g_ve, g_rs, b)
                pool.wait_ge(g_res, 2 * B)

            norm2(0)
            norm2(1)
            pool.wait_ge(t_su, 2)
            for c in MANY_WEIGHTS:
                times_A(fs, tsu[:, :, SEG - CLASSES[c][2]:SEG], c, t_ps)
            norm1(3)
            for c, (_, _, w, _) in enumerate(CLASSES):
                pool.wait_ge(t_a, c + 1)
                pool.memset(flat(fa, c)[:, 0::w], 0.0).then_inc(t_a0, 1)

            def weight_C(q):
                c, i = CHUNKS[q]
                pool.wait_ge(t_s, c + 1)
                pool.wait_ge(t_cs, q + 1)
                v = chunk(fs, c, i)
                pool.tensor_tensor(v, v, cs[:, q % 2, 0:v.shape[1]], ALU.mult).then_inc(t_cw, 1)

            def weigh(c):
                pool.wait_ge(t_h, SCANS.index(c) + 1)
                pool.wait_ge(t_cw, sum(q <= c for q, _ in CHUNKS))
                pool.tensor_tensor(flat(fv, c), flat(fv, c), flat(fs, c), ALU.mult).then_inc(t_zc, 1)

            def softplus(j):
                v = j + 1
                pool.wait_ge(r_lg, v)
                pool.tensor_scalar(lgr[:, :, :], lg[:, :, :], 0.0, None, ALU.max).then_inc(r_pos, 1)
                pool.wait_ge(r_ex, v)
                pool.tensor_scalar(lgu[:, :, :], lge[:, :, :], 1.0, -1.0, ALU.add, ALU.add).then_inc(r_u, 1)
                pool.wait_ge(r_u, v)
                pool.tensor_scalar(lgu[:, :, :], lgu[:, :, :], TINY, None, ALU.max).then_inc(r_u1, 1)
                pool.wait_ge(r_ln, v)
                pool.tensor_scalar(lgq[:, :, :], lga[:, :, :], TINY, None, ALU.add).then_inc(r_l1, 1)
                pool.wait_ge(r_rc, v)
                pool.wait_ge(r_l1, v)
                pool.tensor_tensor(lgq[:, :, :], lgq[:, :, :], lgu[:, :, :], ALU.mult).then_inc(r_q, 1)
                pool.wait_ge(r_q, v)
                pool.tensor_tensor(lgq[:, :, :], lgq[:, :, :], lge[:, :, :], ALU.mult).then_inc(r_tq, 1)
                pool.wait_ge(r_tq, v)
                pool.wait_ge(r_pos, v)
                pool.tensor_tensor(lgq[:, :, :], lgq[:, :, :], lgr[:, :, :], ALU.add).then_inc(r_spq, 1)
                pool.wait_ge(r_spq, v)
                pool.tensor_scalar(lsp[:, :, :], lgq[:, :, :], LEAST, None, ALU.max).then_inc(r_sp, 1)

            sums = [0]

            def add(dst, a, b):
                pool.tensor_tensor(dst, a, b, ALU.add).then_inc(t_sum, 1)
                sums[0] += 1
                pool.wait_ge(t_sum, sums[0])

            def sum_class(c):
                _, ns, w, _ = CLASSES[c]
                if c > 2:
                    pool.wait_ge(t_zd, c - 2)
                else:
                    pool.wait_ge(t_zc, c + 1)
                v = wide(fv, c)
                n = ns
                while n > 1:
                    n //= 2
                    add(v[:, 0:n], v[:, 0:n], v[:, n:2 * n])
                add(yT[:, :, TAIL - w:TAIL], yT[:, :, TAIL - w:TAIL], v[:, 0])

            softplus(0)
            weight_C(0)
            with_bias(6)
            with_bias(7)
            norm2(2)
            weight_C(1)
            norm2(3)
            weight_C(2)
            weight_C(3)
            norm1(4)
            softplus(1)
            norm1(5)
            weigh(0)
            weight_C(4)
            weight_C(5)
            weight_C(6)
            norm2(4)
            norm2(5)
            weigh(1)
            weight_C(7)
            weight_C(8)
            sum_class(1)
            weigh(2)
            sum_class(2)
            sum_class(3)
            sum_class(4)
            with pool.If(pool.value_load(flag[0:1, 0:1], min_val=0, max_val=1) == GENERAL):
                pool.tensor_copy(yT, gtail[:, :, :]).then_inc(g_yT, 1)
                stop_for(pool, g_yT, 1)
            pool.sem_inc(t_yall, 1)
            softplus(2)
            norm2(6)
            norm2(7)
            softplus(3)

        @block.scalar
        def _(act):
            act.dma_start(wx[:, :], W_x).then_inc(ld_wx, 16)
            act.dma_start(wdt[:, :], W_dt).then_inc(ld_wx, 16)
            act.dma_start(dcol[:, :], col(D)).then_inc(ld_wout, 16)
            act.dma_start(wout[:, :], W_out).then_inc(ld_wout, 16)
            act.dma_start(bdt[:, :], col(b_dt)).then_inc(ld_small, 16)
            act.dma_start(alog[:, :], A_log).then_inc(ld_small, 16)
            act.preload_act_table_set("natural_log_exp_and_others")

            act.wait_ge(wxT_t, 1)
            act.copy(wxT[:, :], bank[0:R, 7, 0:P]).then_inc(wxT_c, 1)
            act.wait_ge(wcomb_p, 1)
            act.copy(wcomb[:, :], bank[:, 2, 0:P]).then_inc(wcomb_c, 1)
            act.wait_ge(ld_small, 32)
            act.activation(aneg[:, :], alog[:, :], ACT.Exp).then_inc(aneg_c, 1)
            act.wait_ge(aneg_c, 1)
            act.mul(aval[:, :], aneg[:, :], -1.0).then_inc(aval_c, 1)

            def turn_out(kind, u, dst):
                act.wait_ge(turned, turn_no(kind, u))
                act.copy(dst, bank[:, 0, :]).then_inc(turn_read, 1)

            def evac1(u):
                past(act, s_o, u - 1)
                turn_out("first", u, xT1[:, u % 2, :, :].rearrange("p t q -> p (t q)"))

            def evac2(u):
                past(act, f_up, NK * (u - 3))
                past(act, r_p, u - 3)
                turn_out("second", u, xT2[:, u % 4, :])

            evac1(0)
            for k in range(2):
                act.wait_ge(t_tp, k + 1)
                act.copy(txT[:, TB // 2 * k:TB // 2 * (k + 1), :].rearrange("p t q -> p (t q)"),
                         bank[:, 5 + k, :]).then_inc(t_xT, 1)

            def half(t, k):
                return t[:, B // 2 * k:B // 2 * (k + 1), :]

            def size(k):
                if k == 0:
                    act.wait_ge(t_z, 1)
                else:
                    act.wait_ge(t_re, 1)
                act.activation(half(tab, k).rearrange("p b w -> p (b w)"), bank[:, 2 + k, :], ACT.Abs,
                               bias=bdt[:, :]).then_inc(t_ab, 1)

            def falling(k):
                act.wait_ge(t_ab, k + 1)
                act.activation(half(tex, k), half(tab, k), ACT.Exp, scale=-1.0).then_inc(t_ex, 1)

            def logarithm(k):
                act.wait_ge(t_ex, k + 1)
                act.activation(half(tab, k), half(tex, k), ACT.Ln, bias=1.0).then_inc(t_ln, 1)

            size(0)
            falling(0)
            size(1)
            falling(1)
            logarithm(0)
            logarithm(1)
            act.wait_ge(t_bcp, 1)
            act.copy(tbc[:, :, :].rearrange("p t n -> p (t n)"), bank[:, 4, 0:TB * 2 * N]).then_inc(t_bc, 1)
            evac1(1)
            evac1(2)

            def per_state(c, dst, src, func, many, multiplied, ready, **bias):
                k0, ns, w, _ = CLASSES[c]
                if c in many:
                    act.wait_ge(multiplied, many.index(c) + 1)
                    op = act.activation(flat(dst, c), flat(dst, c), func, **bias)
                else:
                    for n in range(ns):
                        op = act.activation(wide(dst, c)[:, n], src, func,
                                            scale=aval[:, k0 + n:k0 + n + 1], **bias)
                op.then_inc(ready, 1)

            act.wait_ge(t_dl, 2)
            act.wait_ge(aval_c, 1)
            for c, (_, _, w, _) in enumerate(CLASSES):
                per_state(c, fa, tdl[:, :, TAIL - w:TAIL], ACT.Exp, MANY_DECAYS, t_pa, t_a)
                if c == 1:
                    evac1(3)

            act.wait_ge(t_flag, 1)
            with act.If(act.value_load(flag[0:1, 0:1], min_val=0, max_val=1) == GENERAL):
                with act.Fori(0, B) as b:
                    act.wait_ge(g_tp, b + 1)
                    act.copy(gxT[:, :, :].rearrange("p t q -> p (t q)"), two(0)).then_inc(g_xT, 1)
                    act.wait_ge(g_z, b + 1)
                    act.activation(gre[:, :], two(2), ACT.Relu, bias=bdt[:, :]).then_inc(g_re, 1)
                    act.activation(gab[:, :], two(2), ACT.Abs, bias=bdt[:, :]).then_inc(g_ab, 1)
                    act.wait_ge(g_ab, b + 1)
                    act.activation(gd[:, :], gab[:, :], ACT.Exp, scale=-1.0).then_inc(g_ex, 1)
                    act.wait_ge(g_ex, b + 1)
                    act.activation(gab[:, :], gd[:, :], ACT.Ln, bias=1.0).then_inc(g_ln, 1)
                    act.wait_ge(g_bcp, b + 1)
                    act.copy(gbc[:, :, :].rearrange("p t n -> p (t n)"), bank[:, 4, 0:T * 2 * N])\
                       .then_inc(g_bc, 1)
                    stop_for(act, g_su, b + 1)
                    with act.Fori(0, N) as n:
                        i = N * b + n
                        act.wait_ge(g_col, 3 * i + 3)
                        act.wait_ge(g_h, i + FREE)
                        act.activation(gd[:, :], gdl[:, 0:L], ACT.Exp, scale=gan[:, :]).then_inc(g_a, 1)
                        act.wait_ge(g_hs, i + FREE)
                        act.activation(gs[:, :], gsu[:, 1:L + 1], ACT.Sigmoid, scale=gan[:, :],
                                       bias=logt[:, :]).then_inc(g_s, 1)
                act.wait_ge(g_res, 2 * B)

            act.preload_act_table_set("sigmoid_and_others")
            act.wait_ge(rwT_p, 1)
            act.copy(rwT[:, :], bank[:, 7, 0:E]).then_inc(rwT_c, 1)

            def C_out(q):
                act.wait_ge(t_C, q + 1)
                past(act, t_cw, q - 1)
                n = chunk(fs, *CHUNKS[q]).shape[1]
                act.copy(cs[:, q % 2, 0:n], bank[:, 7, 0:n]).then_inc(t_cs, 1)

            act.wait_ge(t_su, 2)
            act.wait_ge(consts, 5)
            for c, (_, _, w, _) in enumerate(CLASSES):
                per_state(c, fs, tsu[:, :, SEG - w:SEG], ACT.Sigmoid, MANY_WEIGHTS, t_ps, t_s,
                          bias=logt[:, :])
                if c == 0:
                    evac2(0)
                if c == 1:
                    evac2(1)

            def exponents(j):
                v = j + 1
                act.preload_act_table_set("natural_log_exp_and_others")
                act.wait_ge(r_lg, v)
                act.activation(lga[:, :, :], lg[:, :, :], ACT.Abs).then_inc(r_ab, 1)
                act.wait_ge(r_ab, v)
                act.activation(lge[:, :, :], lga[:, :, :], ACT.Exp, scale=-1.0).then_inc(r_ex, 1)
                act.wait_ge(r_ex, v)
                act.activation(lga[:, :, :], lge[:, :, :], ACT.Ln, bias=1.0).then_inc(r_ln, 1)

            def roots(j):
                v = j + 1
                if j:
                    act.preload_act_table_set("natural_log_exp_and_others")
                act.wait_ge(r_sp, v)
                act.activation(lga[:, :, :], lsp[:, :, :], ACT.Ln).then_inc(r_lnsp, 1)
                act.wait_ge(r_lnsp, v)
                act.activation(gact[:, :, :], lga[:, :, :], ACT.Exp, scale=0.5).then_inc(r_act, 1)
                act.preload_act_table_set("silu_and_others")

            def gates_out(u):
                act.wait_ge(turned, turn_no("gates", u))
                past(act, f_cf, NB * (u - 1))
                act.copy(gT[:, u % 2, :], bank[0:GR, 0, :]).then_inc(f_gT, 1)
                past(act, f_dn, u - 1)
                act.copy(gt[H:KX, u % 2, NB, :], bank[0:GR, 0, :]).then_inc(turn_read, 1)

            def silu(u, k):
                act.wait_ge(f_up, NK * u + k + 1)
                src = bank[:, 2 + (NK * u + k) % 2, :]
                if k < NB:
                    past(act, f_g, NB * (u - 1) + k + 1)
                    act.activation(hs[:, k, :], src, ACT.Silu, bias=b1[:, k:k + 1]).then_inc(f_silu, 1)
                else:
                    past(act, f_dn, u - 1)
                    act.activation(gt[0:H, u % 2, k, :], src[0:H, :], ACT.Silu,
                                   bias=b1[0:H, k:k + 1]).then_inc(f_silu, 1)

            act.wait_ge(ld_ffn1, 16 * (NB + 3))
            exponents(0)
            evac1(4)
            C_out(0)
            C_out(1)
            evac1(5)
            roots(0)
            silu(0, 0)
            gates_out(0)
            silu(0, 1)
            silu(0, 2)
            silu(0, 3)
            C_out(2)
            silu(0, 4)
            C_out(3)
            for u in range(1, U):
                ahead = u % 2 and u + 1 < U
                silu(u, 0)
                if ahead:
                    evac2(u + 1)
                if u == 1:
                    C_out(4)
                if u == 2:
                    C_out(7)
                silu(u, 1)
                if ahead:
                    evac2(u + 2)
                    exponents((u + 1) // 2)
                    act.preload_act_table_set("silu_and_others")
                gates_out(u)
                if u == 1:
                    C_out(5)
                if u == 2:
                    C_out(8)
                for k in range(2, NK):
                    silu(u, k)
                if u == 1:
                    C_out(6)
                if ahead:
                    roots((u + 1) // 2)

        @block.tensor
        def _(pe):
            pe.wait_ge(consts, 2)
            pe.wait_ge(ld_wx, 32)
            pe.transpose(bank[0:R, 7, 0:P], wx[:, 0:R], ident[:, :]).then_inc(wxT_t, 1)
            pe.wait_ge(wxT_c, 1)
            pe.matmul(bank[:, 2, 0:P], wxT[:, :], wdt[:, :], start=True, stop=True).then_inc(wcomb_p, 1)
            pe.wait_ge(dwout_c, 1)
            pe.matmul(bank[:, 4, 0:P], average[:, :], dwout[:, :], start=True, stop=True).then_inc(avg_p, 1)

            def turn(kind, u, tile, ready, count):
                pe.wait_ge(ready, count)
                past(pe, turn_read, turn_no(kind, u) - 1)
                for t in range(TH):
                    mm = pe.transpose(bank[:, 0, P * t:P * t + P], tile(t), ident[:, :])
                mm.then_inc(turned, 1)

            def turn1(u):
                turn("first", u, lambda t: unit(xa, u)[:, t, :], ld_x[u // 2], 16 * B)

            def turn2(u):
                turn("second", u, lambda t: xn2[:, u % 2, t, :], n_xn, u + 1)

            def turn_gates(u):
                pe.wait_ge(r_cf, u // 2 + 1)
                pe.wait_ge(turn_read, turn_no("gates", u) - 1)
                for t in range(TH):
                    mm = pe.matmul(bank[0:GR, 0, P * t:P * t + P], g3[:, u // 2 % 2, TH * (u % 2) + t, :],
                                   identb[:, :], start=True, stop=True)
                mm.then_inc(turned, 1)

            def attn_out(u):
                if u < UA:
                    pe.wait_ge(turn_read, turn_no("first", u))
                else:
                    pe.wait_ge(t_own, 1)
                if u != 1:
                    past(pe, s_x1, u)
                for t in range(TH):
                    dst = bank[:, out_bank(u), P * t:P * t + P]
                    if u < UA:
                        mm = pe.matmul(dst, xT1[:, u % 2, t, :], cwout[:, :], start=True, stop=True)
                    else:
                        q = TH * (u - UA) + t
                        mm = pe.matmul(dst, yT[:, q // TT, P * (q % TT):P * (q % TT) + P], wout[:, :],
                                       start=True, stop=True)
                mm.then_inc(s_o, 1)

            turn1(0)
            for k in range(2):
                for j in range(TB // 2):
                    q = TB // 2 * k + j
                    pe.wait_ge(t_xn, q + 1)
                    mm = pe.transpose(bank[:, 5 + k, P * j:P * j + P], txn[:, q, :], ident[:, :])
                mm.then_inc(t_tp, 1)
            pe.wait_ge(wcomb_c, 1)
            for k in range(2):
                pe.wait_ge(t_xT, k + 1)
                pe.matmul(bank[:, 2 + k, :], wcomb[:, :],
                          txT[:, TB // 2 * k:TB // 2 * (k + 1), :].rearrange("p t q -> p (t q)"),
                          start=True, stop=True).then_inc(t_z, 1)
            pe.wait_ge(cwout_c, 1)
            attn_out(0)
            for q in range(TB):
                mm = pe.matmul(bank[:, 4, 2 * N * q:2 * N * (q + 1)], txT[:, q, :], wx[:, R:R + 2 * N],
                               start=True, stop=True)
            mm.then_inc(t_bcp, 1)
            turn1(1)
            attn_out(1)
            turn1(2)
            pe.wait_ge(t_gm, 1)
            pe.transpose(bank[0:1, 7, 0:P], gmax[:, :], ident[:, :]).then_inc(t_gt, 1)
            turn1(3)

            pe.wait_ge(t_flag, 1)
            with pe.If(pe.value_load(flag[0:1, 0:1], min_val=0, max_val=1) == GENERAL):
                pe.wait_ge(turn_read, 4)
                pe.wait_ge(s_x1, 2)
                pe.wait_ge(t_bc, 1)
                with pe.Fori(0, B) as b:
                    pe.wait_ge(g_xn, b + 1)
                    for t in range(T):
                        mm = pe.transpose(banks[:, P * t:P * t + P], gxn[:, t, :], ident[:, :])
                    mm.then_inc(g_tp, 1)
                    pe.wait_ge(g_xT, b + 1)
                    for k in range(2):
                        mm = pe.matmul(bank[:, 2 + k, :], wcomb[:, :],
                                       gxT[:, TH * k:TH * (k + 1), :].rearrange("p t q -> p (t q)"),
                                       start=True, stop=True)
                    mm.then_inc(g_z, 1)
                    for t in range(T):
                        mm = pe.matmul(bank[:, 4, 2 * N * t:2 * N * (t + 1)], gxT[:, t, :],
                                       wx[:, R:R + 2 * N], start=True, stop=True)
                    mm.then_inc(g_bcp, 1)
                    stop_for(pe, g_dl, b + 1)
                    with pe.Fori(0, N) as n:
                        i = N * b + n
                        pe.wait_ge(g_col, 3 * i + 3)
                        pe.wait_ge(g_zc, i + FREE)
                        for s in range(2):
                            for t in range(T):
                                mm = pe.transpose(banks[:, 1024 * (1 + s) + P * t:1024 * (1 + s) + P * t + P],
                                                  gbn[:, s, t:t + 1].to_broadcast([P, P]), ident[:, :])
                        mm.then_inc(g_BC, 1)
                    pe.wait_ge(g_y, N * b + N)
                    for t in range(T):
                        mm = pe.matmul(banks[:, 3072 + P * t:3072 + P * t + P], gy[:, t, :], wout[:, :],
                                       start=True, stop=True)
                    mm.then_inc(g_o, 1)
                pe.wait_ge(g_res, 2 * B)

            def spread(c, column, dst, first, last):
                k0, ns, w, _ = CLASSES[c]
                rows = min(w, P)
                lo = P - rows
                for at in range(first, last, rows):
                    n, b, s = at // w // B, at // w % B, at % w // P
                    src = tbc[lo:P, TT * b + TT - max(1, w // P) + s, column + k0 + n:column + k0 + n + 1]
                    mm = pe.transpose(dst[:, at - first:at - first + rows], src.to_broadcast([rows, P]),
                                      ident[lo:P, lo:P])
                return mm

            def spread_C(q):
                c, i = CHUNKS[q]
                if q:
                    pe.wait_ge(t_cs, q)
                if q in (0, 5):
                    pe.wait_ge(r_lg, 1 + (q == 5))
                spread(c, N, bank[:, 7, :], ROWS * i, min(ROWS * (i + 1), CLASSES[c][1] * B * CLASSES[c][2]))\
                    .then_inc(t_C, 1)

            def router(u):
                pe.wait_ge(turn_read, turn_no("second", u))
                past(pe, r_lg, u // 2)
                if u >= 2:
                    pe.wait_ge(t_cs, 5 if u < 4 else len(CHUNKS))
                at = TH * E * (u % 2)
                for t in range(TH):
                    mm = pe.matmul(bank[:, 7, at + E * t:at + E * t + E], xT2[:, u % 4, P * t:P * t + P],
                                   rwT[:, :], start=True, stop=True)
                mm.then_inc(r_p, 1)

            def up(u, k):
                j = NK * u + k
                m = P if k < NB else H
                past(pe, f_silu, j - 1)
                pe.matmul(bank[0:m, 2 + j % 2, :], w1[:, P * k:P * k + m], xT2[:, u % 4, :],
                          start=True, stop=True).then_inc(f_up, 1)

            def gates_up(u, k):
                j = NB * u + k
                if k == 0:
                    pe.wait_ge(f_gT, u + 1)
                past(pe, f_g, j - 1)
                pe.matmul(bank[:, 4 + j % 2, :],
                          pick[:, EB * k:EB * (k + 1), :].rearrange("p e h -> p (e h)"),
                          gT[:, u % 2, :], start=True, stop=True).then_inc(f_cf, 1)

            def down(u, tiles_of):
                order = (0, 1, NB, *range(2, NB))
                for t in tiles_of:
                    for k in order:
                        if t == 0 and k == order[0]:
                            past(pe, f_out, u)
                        if t == 0 and k == NB:
                            pe.wait_ge(f_silu, NK * (u + 1))
                            pe.wait_ge(turn_read, turn_no("gates", u))
                        elif t == 0:
                            pe.wait_ge(f_g, NB * u + k + 1)
                        rows = P if k < NB else KX
                        mm = pe.matmul(bank[:, down_bank(u, t), P * t:P * t + P],
                                       gt[0:rows, u % 2, k, P * t:P * t + P], w2[0:rows, k, :],
                                       start=(k == order[0]), stop=(k == order[-1]))
                if TH - 1 in tiles_of or u == U - 1:
                    mm.then_inc(f_dn, 1)

            pe.wait_ge(ld_rw, 32)
            pe.transpose(bank[:, 7, 0:E], rw[:, :], ident[0:E, 0:E]).then_inc(rwT_p, 1)
            pe.wait_ge(t_bc, 1)

            def spread_B(c):
                _, ns, w, first = CLASSES[c]
                if c >= 3:
                    pe.wait_ge(t_v, c - 2)
                spread(c, 0, banks[:, ROWS * first:], 0, ns * B * w).then_inc(t_B, 1)

            spread_B(0)
            spread_B(1)
            pe.wait_ge(s_x1, 2)
            spread_B(2)
            attn_out(2)
            turn2(0)
            spread_B(3)
            turn2(1)
            pe.wait_ge(rwT_c, 1)
            router(0)
            router(1)
            turn1(4)
            pe.wait_ge(ld_ffn1, 16 * (NB + 3))
            pe.wait_ge(t_v, 4)
            up(0, 0)
            spread_C(0)
            spread_B(4)
            up(0, 1)
            attn_out(3)
            spread_C(1)
            turn1(5)
            spread_C(2)
            attn_out(4)
            pe.wait_ge(consts2, 2 + E)
            turn_gates(0)
            pe.wait_ge(picked, 3)
            pe.wait_ge(t_v, 5)
            gates_up(0, 0)
            up(0, 2)
            gates_up(0, 1)
            up(0, 3)
            gates_up(0, 2)
            up(0, 4)
            gates_up(0, 3)
            spread_C(3)
            pe.wait_ge(ld_ffn2, 16 * (NB + 5))
            for u in range(1, U):
                ahead = u % 2 and u + 1 < U
                up(u, 0)
                if ahead:
                    turn2(u + 1)
                if u == 1:
                    spread_C(4)
                if u == 2:
                    spread_C(7)
                up(u, 1)
                if ahead:
                    turn2(u + 2)
                if ahead:
                    router(u + 1)
                    router(u + 2)
                if u == UA - 2:
                    attn_out(UA)
                down(u - 1, range(TH // 2))
                if u == UA - 2:
                    attn_out(UA + 1)
                turn_gates(u)
                down(u - 1, range(TH // 2, TH))
                if u == 1:
                    spread_C(5)
                if u == 2:
                    spread_C(8)
                for k in range(NB):
                    gates_up(u, k)
                    if k + 2 < NK:
                        up(u, k + 2)
                if u == 1:
                    attn_out(5)
                    spread_C(6)
            down(U - 1, range(TH // 2))
            down(U - 1, range(TH // 2, TH))

        @block.vector
        def _(dve):
            for used in (g_h, g_hs, g_zc):
                dve.sem_inc(used, FREE)
            half = TB // 2
            for k in range(2):
                dve.wait_ge(ld_tail[k], 16 * B // 2)
                for q in range(half * k, half * (k + 1)):
                    st = dve.bn_stats(tst[:, q, :], xa[:, J - 1, q // TT, q % TT, :])
                st.then_inc(t_st, 1)
                dve.wait_ge(t_st, k + 1)
                for q in range(half * k, half * (k + 1)):
                    mv = dve.bn_aggr(tmv[:, q, :], tst[:, q, :])
                mv.then_inc(t_mv, 1)
            dve.wait_ge(ld_wout, 32)
            dve.tensor_scalar(dwout[:, :], wout[:, :], dcol[:, :], None, ALU.mult).then_inc(dwout_c, 1)

            def moments(u, src, st, mv, slot, stats_done, ready):
                for t in range(TH):
                    q = dve.bn_stats(st[:, slot, t, :], unit(src, u)[:, t, :])
                q.then_inc(stats_done, 1)
                dve.wait_ge(stats_done, u + 1)
                for t in range(TH):
                    q = dve.bn_aggr(mv[:, slot, t, :], st[:, slot, t, :])
                q.then_inc(ready, 1)

            def stats1(u):
                dve.wait_ge(ld_x[u // 2], 16 * B)
                moments(u, xa, st1, mv1, u, s_st, s_mv)

            def stats2(u):
                moments(u, ra, st2, mv2, u % 2, n_st, n_mv)

            def scale2(u):
                if u >= 2:
                    dve.wait_ge(turned, turn_no("second", u - 2))
                dve.wait_ge(n_rs, u + 1)
                for t in range(TH):
                    q = dve.tensor_scalar(xn2[:, u % 2, t, :], unit(ra, u)[:, t, :], mv2[:, u % 2, t, 0:1],
                                          rs2[:, u % 2, t:t + 1], ALU.subtract, ALU.mult)
                q.then_inc(n_xn, 1)

            for q in range(TB):
                if q % half == 0:
                    dve.wait_ge(t_rs, q // half + 1)
                dve.tensor_scalar(txn[:, q, :], xa[:, J - 1, q // TT, q % TT, :], tmv[:, q, 0:1],
                                  trs[:, q:q + 1], ALU.subtract, ALU.mult).then_inc(t_xn, 1)
            dve.wait_ge(avg_p, 1)
            dve.wait_ge(dwout_c, 1)
            dve.tensor_tensor(cwout[:, :], dwout[:, :], bank[:, 4, 0:P], ALU.subtract).then_inc(cwout_c, 1)
            for u in range(4):
                stats1(u)

            def residual1(u):
                dve.wait_ge(s_o, u + 1)
                dve.wait_ge(res_init, u + 1)
                r = unit(ra, u)
                if u < UA:
                    dve.wait_ge(s_rs, u + 1)
                    for t in range(TH):
                        q = dve.scalar_tensor_tensor(out=r[:, t, :],
                                                     in0=bank[:, out_bank(u), P * t:P * t + P],
                                                     scalar=rs1[:, u, t:t + 1], in1=r[:, t, :],
                                                     op0=ALU.mult, op1=ALU.add)
                else:
                    q = dve.tensor_tensor(r, r, bank[:, 1, :].rearrange("p (t q) -> p t q", t=TH), ALU.add)
                q.then_inc(s_x1, 1)
                dve.wait_ge(s_x1, u + 1)

            for k in (1, 0):
                if k:
                    dve.wait_ge(t_z, 2)
                else:
                    dve.wait_ge(t_ab, 1)
                dve.wait_ge(ld_small, 32)
                dve.tensor_scalar(tre[:, B // 2 * k:B // 2 * (k + 1), :].rearrange("p b w -> p (b w)"),
                                  bank[:, 2 + k, :], bdt[:, :], 0.0, ALU.add, ALU.max).then_inc(t_re, 1)
            residual1(0)
            dve.wait_ge(t_re, 2)
            dve.wait_ge(consts, 7)
            for k in range(2):
                seqs = slice(B // 2 * k, B // 2 * (k + 1))
                dve.wait_ge(t_ln, k + 1)
                dve.tensor_tensor(tdl[:, seqs, 0:TAIL], tre[:, seqs, :], tab[:, seqs, :], ALU.add)\
                   .then_inc(t_dl, 1)
                dve.wait_ge(t_dl, k + 1)
                backwards = slice(B // 2 * SEG - 1, None, -1)
                dve.tensor_tensor_scan(tsu[:, seqs, :].rearrange("p b w -> p (b w)")[:, backwards],
                                       mask[:, backwards],
                                       tdl[:, seqs, :].rearrange("p b w -> p (b w)")[:, backwards], 0.0,
                                       ALU.mult, ALU.add).then_inc(t_su, 1)
            dve.wait_ge(t_su, 2)
            dve.wait_ge(aval_c, 1)
            for k0, ns, w, _ in CLASSES:
                gp = dve.tensor_tensor(gprod[:, k0:k0 + ns, :],
                                       aval[:, k0:k0 + ns].unsqueeze(2).to_broadcast([P, ns, B]),
                                       tsu[:, :, TAIL - w].unsqueeze(1).to_broadcast([P, ns, B]), ALU.mult)
            gp.then_inc(t_gp, 1)
            dve.wait_ge(t_gp, 1)
            dve.tensor_reduce(gmax[:, :], gprod[:, :, :].rearrange("p n b -> p (n b)"), AX.X, ALU.max)\
               .then_inc(t_gm, 1)
            dve.wait_ge(t_gt, 1)
            dve.tensor_reduce(gmx1[:, :], bank[0:1, 7, 0:P], AX.X, ALU.max).then_inc(t_g1, 1)
            dve.wait_ge(t_g1, 1)
            dve.tensor_scalar(flag[:, :], gmx1[:, :], UNDERFLOW, None, ALU.is_ge).then_inc(t_flag, 1)

            residual1(1)

            dve.wait_ge(t_flag, 1)
            with dve.If(dve.value_load(flag[0:1, 0:1], min_val=0, max_val=1) == GENERAL):
                for j in range(J - 1):
                    dve.wait_ge(ld_x[j], 16 * B)
                dve.wait_ge(res_init, UA)
                dve.memset(gdl[:, L:L + 1], 0.0).then_inc(g_zero, 1)
                with dve.Fori(0, B) as b:
                    for t in range(T):
                        dve.bn_stats(gst[:, t, :], xa[:, t // TT, b, t % TT, :]).then_inc(g_st, 1)
                    stop_for(dve, g_st, T * b + T)
                    for t in range(T):
                        mv = dve.bn_aggr(gmv[:, t, :], gst[:, t, :])
                    mv.then_inc(g_mv, 1)
                    dve.wait_ge(g_rs, b + 1)
                    for t in range(T):
                        xn = dve.tensor_scalar(gxn[:, t, :], xa[:, t // TT, b, t % TT, :], gmv[:, t, 0:1],
                                               grs[:, t:t + 1], ALU.subtract, ALU.mult)
                    xn.then_inc(g_xn, 1)
                    dve.wait_ge(g_ln, b + 1)
                    dve.wait_ge(g_re, b + 1)
                    dve.tensor_tensor(gdl[:, 0:L], gre[:, :], gab[:, :], ALU.add).then_inc(g_dl, 1)
                    dve.wait_ge(g_dl, b + 1)
                    dve.wait_ge(g_zero, b + 1)
                    dve.tensor_tensor_scan(gsu[:, ::-1], mask[:, 0:1].to_broadcast([P, L + 1]),
                                           gdl[:, ::-1], 0.0, ALU.mult, ALU.add).then_inc(g_su, 1)
                    dve.tensor_tensor(gw[:, :], gdl[:, 0:L], gxT[:, :, :].rearrange("p t q -> p (t q)"),
                                      ALU.mult).then_inc(g_w, 1)
                    dve.memset(gy[:, :, :], 0.0).then_inc(g_zero, 1)
                    dve.wait_ge(g_zero, b + 2)
                    dve.wait_ge(g_bc, b + 1)
                    stop_for(dve, g_w, b + 1)
                    with dve.Fori(0, N) as n:
                        i = N * b + n
                        dve.tensor_copy(gbn[:, 0, :], gbc[:, :, n]).then_inc(g_col, 1)
                        dve.tensor_copy(gbn[:, 1, :], gbc[:, :, N + n]).then_inc(g_col, 1)
                        dve.tensor_copy(gan[:, :], aval[:, bass.ds(n, 1)]).then_inc(g_col, 1)
                        dve.wait_ge(g_BC, i + 1)
                        dve.tensor_tensor(gv[:, :], gw[:, :], two(2), ALU.mult).then_inc(g_v, 1)
                        dve.wait_ge(g_v, i + 1)
                        dve.wait_ge(g_a, i + 1)
                        dve.tensor_tensor_scan(gh[:, :], gd[:, :], gv[:, :], 0.0, ALU.mult, ALU.add)\
                           .then_inc(g_h, 1)
                        dve.wait_ge(g_h, i + 1 + FREE)
                        dve.wait_ge(g_s, i + 1)
                        dve.tensor_tensor(gv[:, :], gh[:, :], gs[:, :], ALU.mult).then_inc(g_hs, 1)
                        dve.wait_ge(g_hs, i + 1 + FREE)
                        dve.tensor_tensor(gh[:, :], gv[:, :], two(4), ALU.mult).then_inc(g_zc, 1)
                        dve.wait_ge(g_zc, i + 1 + FREE)
                        dve.tensor_tensor(gy[:, :, :].rearrange("p t q -> p (t q)"),
                                          gy[:, :, :].rearrange("p t q -> p (t q)"), gh[:, :],
                                          ALU.add).then_inc(g_y, 1)
                        dve.wait_ge(g_y, i + 1)
                    dve.wait_ge(g_o, b + 1)
                    earlier = ra[:, 0:J - 1, b, :, :].rearrange("p j s d -> p j (s d)")
                    dve.tensor_tensor(earlier, earlier,
                                      banks[:, 3072:3072 + P * (T - TT)].rearrange("p (j n) -> p j n", j=J - 1),
                                      ALU.add).then_inc(g_res, 1)
                    dve.tensor_copy(gtail[:, b, :], gy[:, T - TT:T, :].rearrange("p t q -> p (t q)"))\
                       .then_inc(g_res, 1)
                    stop_for(dve, g_res, 2 * b + 2)

            def scan_inputs(c):
                _, ns, w, _ = CLASSES[c]
                dve.wait_ge(t_w, 1)
                dve.wait_ge(t_B, c + 1)
                dve.tensor_tensor(wide(fv, c), psum_class(c).rearrange("p (n b w) -> p n b w", n=ns, b=B),
                                  tw[:, :, TAIL - w:TAIL].unsqueeze(1).to_broadcast([P, ns, B, w]),
                                  ALU.mult).then_inc(t_v, 1)

            def scan(c):
                dve.wait_ge(t_v, c + 1)
                dve.wait_ge(t_a0, c + 1)
                dve.tensor_tensor_scan(flat(fv, c), flat(fa, c), flat(fv, c), 0.0, ALU.mult, ALU.add)\
                   .then_inc(t_h, 1)

            def over_experts(t):
                return t[:, :].unsqueeze(2).to_broadcast([P, T, E])

            def small(op, dst, a, b, ready, v):
                dve.tensor_tensor(dst[:, :, :], a, b, op).then_inc(ready, 1)
                dve.wait_ge(ready, v)

            def most(dst, src, ready, v):
                dve.tensor_reduce(dst[:, :], src[:, :, :], AX.X, ALU.max).then_inc(ready, 1)
                dve.wait_ge(ready, v)

            def invert(j):
                dve.wait_ge(r_u1, j + 1)
                dve.reciprocal(lgu[:, :, :], lgu[:, :, :]).then_inc(r_rc, 1)

            def choose(j):
                v = j + 1
                ramps = ramp[:, :].unsqueeze(1).to_broadcast([P, T, E])
                dve.wait_ge(r_p, 2 * v)
                past(dve, r_sp, j)
                small(ALU.add, lg, bank[:, 7, 0:T * E].rearrange("p (t e) -> p t e", e=E),
                      ebias[:, :].unsqueeze(1).to_broadcast([P, T, E]), r_lg, v)
                most(m1, lg, r_m1, v)
                small(ALU.is_equal, oh1, lg[:, :, :], over_experts(m1), r_eq1, v)
                small(ALU.mult, oh2, oh1[:, :, :], ramps, r_w1, v)
                most(p1, oh2, r_p1, v)
                small(ALU.is_equal, oh1, ramps, over_experts(p1), r_oh1, v)
                dve.scalar_tensor_tensor(out=rest[:, :, :], in0=oh1[:, :, :], scalar=TAKEN,
                                         in1=lg[:, :, :], op0=ALU.mult, op1=ALU.add).then_inc(r_rest, 1)
                dve.wait_ge(r_rest, v)
                most(m1, rest, r_m2, v)
                if j <= 1:
                    invert(j)
                small(ALU.is_equal, oh2, rest[:, :, :], over_experts(m1), r_eq2, v)
                small(ALU.mult, rest, oh2[:, :, :], ramps, r_w2, v)
                most(p1, rest, r_p2, v)
                small(ALU.is_equal, oh2, ramps, over_experts(p1), r_oh2, v)
                small(ALU.add, oh1, oh1[:, :, :], oh2[:, :, :], r_sel, v)

            def settle(j):
                v = j + 1
                dve.wait_ge(r_act, v)
                small(ALU.mult, gval, oh1[:, :, :], gact[:, :, :], r_val, v)
                if j >= 2:
                    dve.wait_ge(turned, turn_no("gates", 2 * j - 3))
                part = [g3[:, j % 2, :, E * i:E * (i + 1)] for i in range(3)]
                dve.tensor_copy(part[0], gval[:, :, :]).then_inc(r_hi, 1)
                dve.wait_ge(r_hi, v)
                small(ALU.subtract, grest, gval[:, :, :], part[0], r_rem, v)
                dve.tensor_copy(part[1], grest[:, :, :]).then_inc(r_mid, 1)
                dve.wait_ge(r_mid, v)
                dve.tensor_tensor(part[2], grest[:, :, :], part[1], ALU.subtract).then_inc(r_cf, 1)

            def gate(u, k):
                j = NB * u + k
                past(dve, f_dn, u - 1)
                dve.wait_ge(f_cf, j + 1)
                dve.wait_ge(f_silu, NK * u + k + 1)
                dve.tensor_tensor(gt[:, u % 2, k, :], hs[:, k, :], bank[:, 4 + j % 2, :], ALU.mult)\
                   .then_inc(f_g, 1)

            def weigh(c):
                dve.wait_ge(t_h, SCANS.index(c) + 1)
                dve.wait_ge(t_cw, sum(q <= c for q, _ in CHUNKS))
                dve.tensor_tensor(flat(fv, c), flat(fv, c), flat(fs, c), ALU.mult).then_inc(t_zd, 1)

            def residual2(u):
                dve.wait_ge(f_dn, u + 1)
                past(dve, stored[u % 2], 16 * B // 2 * (u // 2))
                dve.tensor_tensor(yo[:, u % 2, :, :], unit(ra, u),
                                  bank[:, 6, :].rearrange("p (t q) -> p t q", t=TH), ALU.add)\
                   .then_inc(f_out, 1)

            stats2(0)
            stats2(1)
            scale2(0)
            scan_inputs(0)
            scale2(1)
            scan_inputs(1)
            scan_inputs(2)
            scan_inputs(3)
            residual1(2)
            dve.wait_ge(ld_rw, 32)
            dve.wait_ge(consts2, 1 + E)
            choose(0)
            residual1(3)
            settle(0)
            scan_inputs(4)
            stats2(2)
            gate(0, 0)
            gate(0, 1)
            stats2(3)
            gate(0, 2)
            scale2(2)
            gate(0, 3)
            scale2(3)
            stats1(4)
            scan(0)
            stats1(5)
            scan(3)
            choose(1)
            residual2(0)
            gate(1, 0)
            residual1(4)
            gate(1, 1)
            gate(1, 2)
            gate(1, 3)
            settle(1)
            stats2(4)
            residual1(5)
            stats2(5)
            scan(1)
            scan(2)
            for u in range(2, U):
                ahead = u % 2 and u + 1 < U
                if ahead:
                    choose((u + 1) // 2)
                if u == UA - 2:
                    residual1(UA)
                    stats2(UA)
                    residual1(UA + 1)
                    stats2(UA + 1)
                residual2(u - 1)
                for k in range(NB):
                    if k == NB - 1 and u in (2, UA - 2):
                        scale2(u + 2)
                        scale2(u + 3)
                    gate(u, k)
                    if u == UA - 3 and k == 1:
                        dve.wait_ge(t_yall, 1)
                        dve.scalar_tensor_tensor(out=yT.rearrange("p b w -> p (b w)"),
                                                 in0=txT[:, :, :].rearrange("p t q -> p (t q)"),
                                                 scalar=dcol[:, :], in1=yT.rearrange("p b w -> p (b w)"),
                                                 op0=ALU.mult, op1=ALU.add).then_inc(t_own, 1)
                    if ahead and k == 1:
                        invert((u + 1) // 2)
                if ahead:
                    settle((u + 1) // 2)
                if u == 2:
                    scan(4)
                    weigh(3)
                    weigh(4)
            dve.wait_ge(stored[(U - 1) % 2], 16 * B // 2 * ((U - 1) // 2))
            for k in range(2):
                dve.wait_ge(f_dn, U + k)
                part = slice(TT * k, TT * (k + 1))
                dve.tensor_tensor(yo[:, (U - 1) % 2, part, :], unit(ra, U - 1)[:, part, :],
                                  bank[:, down_bank(U - 1, TT * k), P * TT * k:P * TT * (k + 1)]
                                  .rearrange("p (t q) -> p t q", t=TT), ALU.add).then_inc(f_out, 1)


_INS = ['L0_attn_x', 'L0_attn_W_x', 'L0_attn_W_dt', 'L0_attn_b_dt', 'L0_attn_A_log', 'L0_attn_D',
        'L0_attn_W_out', 'L0_attn_b_out', 'L0_ffn_routing_W', 'L0_ffn_expert_bias', 'L0_ffn_sW1',
        'L0_ffn_sb1', 'L0_ffn_sW2', 'L0_ffn_sb2', 'L0_ffn_rW1', 'L0_ffn_rb1', 'L0_ffn_rW2', 'L0_ffn_rb2']


def kernel(**inputs):
    import numpy as np
    import concourse.bacc as bacc
    from concourse import mybir as mb
    from concourse.bass_utils import run_bass_kernel_spmd

    nc = bacc.Bacc("TRN2", target_bir_lowering=False, num_devices=1)
    arrays, args = {}, []
    for name in _INS:
        a = np.ascontiguousarray(inputs[name])
        arrays[f"in_{name}"] = a
        args.append(nc.dram_tensor(f"in_{name}", a.shape, mb.dt.from_np(a.dtype), kind="ExternalInput").ap())
    shape = arrays["in_L0_attn_x"].shape
    args.append(nc.dram_tensor("out", shape, mb.dt.float32, kind="ExternalOutput").ap())
    build(nc, *args)
    r = run_bass_kernel_spmd(nc, [arrays], core_ids=[0])
    return r.results[0]["out"]
```
